# Optimizing a Trainium2 kernel written in Bass

```python
import numpy as np
import jax
import jax.numpy as jnp

def _softmax(x, axis=-1):
    return jax.nn.softmax(x, axis=axis)

def _gelu(x):
    return jax.nn.gelu(x, approximate=True)

def _silu(x):
    return jax.nn.silu(x)

def _sigmoid(x):
    return jax.nn.sigmoid(x)

def _layernorm(x, axis=-1, eps=1e-05):
    m = jnp.mean(x, axis=axis, keepdims=True)
    v = jnp.var(x, axis=axis, keepdims=True)
    return (x - m) / jnp.sqrt(v + eps)

def _scatter_add(tgt, idx, src, axis=0):
    return tgt.at[idx].add(src)

def _segment_sum(src, seg, n):
    return jax.ops.segment_sum(src, seg, n)
kernel_name = 'mk_gnn_resnorm_d2_gnn_r32_7e04f8'

def setup_inputs(seed: int=0):
    np.random.seed(seed)
    _w = jnp.asarray

    def _rec_inputs():
        import jax
        import jax.numpy as jnp
        _gk = jax.random.key(seed)
        x = -0.000202 + 1 * jax.random.normal(jax.random.fold_in(_gk, 1), (3125, 128), jnp.float32)
        _s = jax.random.randint(jax.random.fold_in(_gk, 2), (25000,), 0, 3125, jnp.int32)
        _d = jax.random.randint(jax.random.fold_in(_gk, 3), (25000,), 0, 3125, jnp.int32)
        _loop = jnp.arange(3125, dtype=jnp.int32)
        src = jnp.concatenate([_s, _d, _loop])
        dst = jnp.concatenate([_d, _s, _loop])
        _o = jnp.argsort(dst, stable=True)
        src = src[_o]
        dst = dst[_o]
        edge_attr_64 = 0.000189758 + 1.00013 * jax.random.normal(jax.random.fold_in(_gk, 11), (53125, 64), jnp.float32)
        return (x, src, dst, edge_attr_64)
    x, src, dst, edge_attr_64 = _rec_inputs()

    def _L0_gnn_setup():
        import jax, jax.numpy as jnp
        import numpy as np
        N = 50000
        E = 25000
        HID = 128
        NH = 8
        HD = 16
        FFN = 512
        EPS = 1e-05

        def _layer_norm(x, g, b):
            m = jnp.mean(x, axis=-1, keepdims=True)
            v = jnp.mean((x - m) ** 2, axis=-1, keepdims=True)
            return (x - m) * jax.lax.rsqrt(v + EPS) * g + b

        def _gnn_layer(x, edge_index, Wq, bq, Wk, bk, Wv, bv, Wo, bo, g1, b1, g2, b2, W1, bf1, W2, bf2):
            n = x.shape[0]
            residual = x
            h = _layer_norm(x, g1, b1)
            q = (h @ Wq + bq).reshape(n, NH, HD)
            k = (h @ Wk + bk).reshape(n, NH, HD)
            v = (h @ Wv + bv).reshape(n, NH, HD)
            src, dst = (edge_index[0], edge_index[1])
            deg = jax.ops.segment_sum(jnp.ones(src.shape, x.dtype), dst, num_segments=n)
            loops = jnp.arange(n, dtype=src.dtype)
            s_all = jnp.concatenate([src, loops])
            d_all = jnp.concatenate([dst, loops])
            e = jnp.sum(q[d_all] * k[s_all], axis=-1) / np.sqrt(HD).astype(np.float32)
            m = jax.lax.stop_gradient(jax.ops.segment_max(e, d_all, num_segments=n))
            p = jnp.exp(e - m[d_all])
            z = jax.ops.segment_sum(p, d_all, num_segments=n)
            alpha = p / z[d_all]
            agg = jax.ops.segment_sum(alpha[:, :, None] * v[s_all], d_all, num_segments=n)
            agg = jnp.where(deg[:, None, None] > 0, agg, jnp.zeros_like(agg))
            att = agg.reshape(n, NH * HD) @ Wo + bo
            x = residual + att
            residual = x
            h = _layer_norm(x, g2, b2)
            ffn = jax.nn.gelu(h @ W1 + bf1, approximate=False) @ W2 + bf2
            return residual + ffn
        key = jax.random.key(seed)
        ks = jax.random.split(key, 12)
        s = 0.02
        d = {}
        d['x'] = jax.random.normal(ks[0], (N, HID), jnp.float32)
        d['edge_index'] = jax.random.randint(ks[1], (2, E), 0, N, dtype=jnp.int32)
        d['Wq'] = jax.random.normal(ks[2], (HID, NH * HD), jnp.float32) * s
        d['bq'] = jnp.zeros((NH * HD,), jnp.float32)
        d['Wk'] = jax.random.normal(ks[3], (HID, NH * HD), jnp.float32) * s
        d['bk'] = jnp.zeros((NH * HD,), jnp.float32)
        d['Wv'] = jax.random.normal(ks[4], (HID, NH * HD), jnp.float32) * s
        d['bv'] = jnp.zeros((NH * HD,), jnp.float32)
        d['Wo'] = jax.random.normal(ks[5], (NH * HD, HID), jnp.float32) * s
        d['bo'] = jnp.zeros((HID,), jnp.float32)
        d['g1'] = jnp.ones((HID,), jnp.float32)
        d['b1'] = jnp.zeros((HID,), jnp.float32)
        d['g2'] = jnp.ones((HID,), jnp.float32)
        d['b2'] = jnp.zeros((HID,), jnp.float32)
        d['W1'] = jax.random.normal(ks[6], (HID, FFN), jnp.float32) * s
        d['bf1'] = jnp.zeros((FFN,), jnp.float32)
        d['W2'] = jax.random.normal(ks[7], (FFN, HID), jnp.float32) * s
        d['bf2'] = jnp.zeros((HID,), jnp.float32)
        return d
    _L0_gnn_all = _L0_gnn_setup()
    _L0_gnn_in = {k: v for k, v in _L0_gnn_all.items() if k in ('Wq', 'bq', 'Wk', 'bk', 'Wv', 'bv', 'Wo', 'bo', 'g1', 'b1', 'g2', 'b2', 'W1', 'bf1', 'W2', 'bf2')}
    del _L0_gnn_all

    def _L1_gnn_setup():
        import jax, jax.numpy as jnp
        import numpy as np
        N, E, D, H, ED = (50000, 25000, 128, 8, 64)
        C = D // H

        def _ln(x, g, b, eps=1e-05):
            m = jnp.mean(x, axis=-1, keepdims=True)
            v = jnp.var(x, axis=-1, keepdims=True)
            return (x - m) * jax.lax.rsqrt(v + eps) * g + b
        key = jax.random.key(seed)
        ks = jax.random.split(key, 16)
        p = lambda k, shape: jax.random.normal(k, shape, dtype=jnp.float32) * 0.05
        return {'x': jax.random.normal(ks[0], (N, D), dtype=jnp.float32), 'edge_index': jax.random.randint(ks[1], (2, E), 0, N, dtype=jnp.int64), 'edge_attr': jax.random.normal(ks[2], (E, ED), dtype=jnp.float32), 'Wq': p(ks[3], (D, D)), 'bq': jnp.zeros((D,), jnp.float32), 'Wk': p(ks[4], (D, D)), 'bk': jnp.zeros((D,), jnp.float32), 'Wv': p(ks[5], (D, D)), 'bv': jnp.zeros((D,), jnp.float32), 'We': p(ks[6], (ED, D)), 'Wskip': p(ks[7], (D, D)), 'bskip': jnp.zeros((D,), jnp.float32), 'g1': jnp.ones((D,), jnp.float32), 'b1': jnp.zeros((D,), jnp.float32), 'g2': jnp.ones((D,), jnp.float32), 'b2': jnp.zeros((D,), jnp.float32), 'Wf1': p(ks[8], (D, 4 * D)), 'bf1': jnp.zeros((4 * D,), jnp.float32), 'Wf2': p(ks[9], (4 * D, D)), 'bf2': jnp.zeros((D,), jnp.float32)}
    _L1_gnn_all = _L1_gnn_setup()
    _L1_gnn_in = {k: v for k, v in _L1_gnn_all.items() if k in ('Wq', 'bq', 'Wk', 'bk', 'Wv', 'bv', 'We', 'Wskip', 'bskip', 'g1', 'b1', 'g2', 'b2', 'Wf1', 'bf1', 'Wf2', 'bf2')}
    del _L1_gnn_all
    return {'x': x, 'src': src, 'dst': dst, 'edge_attr_64': edge_attr_64, 'L0_gnn_Wq': _L0_gnn_in['Wq'], 'L0_gnn_bq': _L0_gnn_in['bq'], 'L0_gnn_Wk': _L0_gnn_in['Wk'], 'L0_gnn_bk': _L0_gnn_in['bk'], 'L0_gnn_Wv': _L0_gnn_in['Wv'], 'L0_gnn_bv': _L0_gnn_in['bv'], 'L0_gnn_Wo': _L0_gnn_in['Wo'], 'L0_gnn_bo': _L0_gnn_in['bo'], 'L0_gnn_g1': _L0_gnn_in['g1'], 'L0_gnn_b1': _L0_gnn_in['b1'], 'L0_gnn_g2': _L0_gnn_in['g2'], 'L0_gnn_b2': _L0_gnn_in['b2'], 'L0_gnn_W1': _L0_gnn_in['W1'], 'L0_gnn_bf1': _L0_gnn_in['bf1'], 'L0_gnn_W2': _L0_gnn_in['W2'], 'L0_gnn_bf2': _L0_gnn_in['bf2'], 'L1_gnn_Wq': _L1_gnn_in['Wq'], 'L1_gnn_bq': _L1_gnn_in['bq'], 'L1_gnn_Wk': _L1_gnn_in['Wk'], 'L1_gnn_bk': _L1_gnn_in['bk'], 'L1_gnn_Wv': _L1_gnn_in['Wv'], 'L1_gnn_bv': _L1_gnn_in['bv'], 'L1_gnn_We': _L1_gnn_in['We'], 'L1_gnn_Wskip': _L1_gnn_in['Wskip'], 'L1_gnn_bskip': _L1_gnn_in['bskip'], 'L1_gnn_g1': _L1_gnn_in['g1'], 'L1_gnn_b1': _L1_gnn_in['b1'], 'L1_gnn_g2': _L1_gnn_in['g2'], 'L1_gnn_b2': _L1_gnn_in['b2'], 'L1_gnn_Wf1': _L1_gnn_in['Wf1'], 'L1_gnn_bf1': _L1_gnn_in['bf1'], 'L1_gnn_Wf2': _L1_gnn_in['Wf2'], 'L1_gnn_bf2': _L1_gnn_in['bf2']}

def reference(x, src, dst, edge_attr_64, L0_gnn_Wq, L0_gnn_bq, L0_gnn_Wk, L0_gnn_bk, L0_gnn_Wv, L0_gnn_bv, L0_gnn_Wo, L0_gnn_bo, L0_gnn_g1, L0_gnn_b1, L0_gnn_g2, L0_gnn_b2, L0_gnn_W1, L0_gnn_bf1, L0_gnn_W2, L0_gnn_bf2, L1_gnn_Wq, L1_gnn_bq, L1_gnn_Wk, L1_gnn_bk, L1_gnn_Wv, L1_gnn_bv, L1_gnn_We, L1_gnn_Wskip, L1_gnn_bskip, L1_gnn_g1, L1_gnn_b1, L1_gnn_g2, L1_gnn_b2, L1_gnn_Wf1, L1_gnn_bf1, L1_gnn_Wf2, L1_gnn_bf2):
    import jax
    import jax.numpy as jnp

    def _L0_gnn_ref(x, edge_index, Wq, bq, Wk, bk, Wv, bv, Wo, bo, g1, b1, g2, b2, W1, bf1, W2, bf2):
        import jax, jax.numpy as jnp
        import numpy as np
        N = 50000
        E = 25000
        HID = 128
        NH = 8
        HD = 16
        FFN = 512
        EPS = 1e-05

        def _layer_norm(x, g, b):
            m = jnp.mean(x, axis=-1, keepdims=True)
            v = jnp.mean((x - m) ** 2, axis=-1, keepdims=True)
            return (x - m) * jax.lax.rsqrt(v + EPS) * g + b

        def _gnn_layer(x, edge_index, Wq, bq, Wk, bk, Wv, bv, Wo, bo, g1, b1, g2, b2, W1, bf1, W2, bf2):
            n = x.shape[0]
            residual = x
            h = _layer_norm(x, g1, b1)
            q = (h @ Wq + bq).reshape(n, NH, HD)
            k = (h @ Wk + bk).reshape(n, NH, HD)
            v = (h @ Wv + bv).reshape(n, NH, HD)
            src, dst = (edge_index[0], edge_index[1])
            deg = jax.ops.segment_sum(jnp.ones(src.shape, x.dtype), dst, num_segments=n)
            loops = jnp.arange(n, dtype=src.dtype)
            s_all = jnp.concatenate([src, loops])
            d_all = jnp.concatenate([dst, loops])
            e = jnp.sum(q[d_all] * k[s_all], axis=-1) / np.sqrt(HD).astype(np.float32)
            m = jax.lax.stop_gradient(jax.ops.segment_max(e, d_all, num_segments=n))
            p = jnp.exp(e - m[d_all])
            z = jax.ops.segment_sum(p, d_all, num_segments=n)
            alpha = p / z[d_all]
            agg = jax.ops.segment_sum(alpha[:, :, None] * v[s_all], d_all, num_segments=n)
            agg = jnp.where(deg[:, None, None] > 0, agg, jnp.zeros_like(agg))
            att = agg.reshape(n, NH * HD) @ Wo + bo
            x = residual + att
            residual = x
            h = _layer_norm(x, g2, b2)
            ffn = jax.nn.gelu(h @ W1 + bf1, approximate=False) @ W2 + bf2
            return residual + ffn
        return _gnn_layer(x, edge_index, Wq, bq, Wk, bk, Wv, bv, Wo, bo, g1, b1, g2, b2, W1, bf1, W2, bf2)

    def _L1_gnn_ref(x, edge_index, edge_attr, Wq, bq, Wk, bk, Wv, bv, We, Wskip, bskip, g1, b1, g2, b2, Wf1, bf1, Wf2, bf2):
        import jax, jax.numpy as jnp
        import numpy as np
        N, E, D, H, ED = (50000, 25000, 128, 8, 64)
        C = D // H

        def _ln(x, g, b, eps=1e-05):
            m = jnp.mean(x, axis=-1, keepdims=True)
            v = jnp.var(x, axis=-1, keepdims=True)
            return (x - m) * jax.lax.rsqrt(v + eps) * g + b
        n = x.shape[0]
        src, dst = (edge_index[0], edge_index[1])
        q = (x @ Wq + bq).reshape(n, H, C)
        k = (x @ Wk + bk).reshape(n, H, C)
        v = (x @ Wv + bv).reshape(n, H, C)
        e = (edge_attr @ We).reshape(-1, H, C)
        k_j = k[src] + e
        v_j = v[src] + e
        logits = jnp.sum(q[dst] * k_j, axis=-1) / np.sqrt(C)
        m = jax.ops.segment_max(logits, dst, num_segments=n)
        ex = jnp.exp(logits - m[dst])
        denom = jax.ops.segment_sum(ex, dst, num_segments=n)
        alpha = ex / denom[dst]
        agg = jax.ops.segment_sum(alpha[..., None] * v_j, dst, num_segments=n)
        conv = agg.reshape(n, D) + x @ Wskip + bskip
        h = _ln(conv + x, g1, b1)
        ffn = jax.nn.gelu(h @ Wf1 + bf1, approximate=False) @ Wf2 + bf2
        return _ln(ffn + h, g2, b2)
    edge_index = jnp.stack([src, dst])
    x = _layernorm(x + _L0_gnn_ref(x, edge_index, L0_gnn_Wq, L0_gnn_bq, L0_gnn_Wk, L0_gnn_bk, L0_gnn_Wv, L0_gnn_bv, L0_gnn_Wo, L0_gnn_bo, L0_gnn_g1, L0_gnn_b1, L0_gnn_g2, L0_gnn_b2, L0_gnn_W1, L0_gnn_bf1, L0_gnn_W2, L0_gnn_bf2), axis=-1)
    x = _layernorm(x + _L1_gnn_ref(x, edge_index, edge_attr_64, L1_gnn_Wq, L1_gnn_bq, L1_gnn_Wk, L1_gnn_bk, L1_gnn_Wv, L1_gnn_bv, L1_gnn_We, L1_gnn_Wskip, L1_gnn_bskip, L1_gnn_g1, L1_gnn_b1, L1_gnn_g2, L1_gnn_b2, L1_gnn_Wf1, L1_gnn_bf1, L1_gnn_Wf2, L1_gnn_bf2), axis=-1)
    return x

_drawn_inputs = setup_inputs


def setup_inputs(seed=0):
    import zlib

    import numpy as np

    out = dict(_drawn_inputs(seed))
    spreads = {'L0_gnn_bq': (0.0, 0.8),
     'L0_gnn_bk': (0.0, 2.0),
     'L0_gnn_bv': (0.0, 0.695),
     'L0_gnn_bo': (0.0, 0.1),
     'L0_gnn_g1': (1.0, 0.6),
     'L0_gnn_b1': (0.0, 0.8),
     'L0_gnn_g2': (1.0, 0.6),
     'L0_gnn_b2': (0.0, 2.0),
     'L0_gnn_bf1': (0.0, 0.599),
     'L0_gnn_bf2': (0.0, 0.1),
     'L1_gnn_bq': (0.0, 0.8),
     'L1_gnn_bk': (0.0, 2.0),
     'L1_gnn_bv': (0.0, 0.1),
     'L1_gnn_bskip': (0.0, 0.1),
     'L1_gnn_g1': (1.0, 0.2),
     'L1_gnn_b1': (0.0, 0.1),
     'L1_gnn_g2': (1.0, 0.2),
     'L1_gnn_b2': (0.0, 0.1),
     'L1_gnn_bf1': (0.0, 0.1),
     'L1_gnn_bf2': (0.0, 0.1)}
    factors = {'L0_gnn_Wq': 8.0, 'L0_gnn_Wk': 8.0, 'L0_gnn_Wv': 7.557, 'L0_gnn_Wo': 4.105}
    for name, (base, spread) in spreads.items():
        noise = np.random.default_rng([zlib.crc32(name.encode()), seed]).standard_normal(out[name].shape)
        drawn = base * np.exp(spread * noise) if base else spread * noise
        out[name] = jnp.asarray(drawn.astype(out[name].dtype))
    for name, factor in factors.items():
        out[name] = (out[name] * factor).astype(out[name].dtype)
    return out
```

```python
from contextlib import ExitStack

import concourse.bass as bass
from concourse import mybir

F32 = mybir.dt.float32
BF16 = mybir.dt.bfloat16
I32 = mybir.dt.int32
U32 = mybir.dt.uint32
U8 = mybir.dt.uint8
ACT = mybir.ActivationFunctionType
ALU = mybir.AluOpType
AX = mybir.AxisListType
ds = bass.ds

P = 128
N = 3125
E = 53125
D = 128
H = 8
C = D // H
FF = 512
ED = 64
NB = 26
NP = NB * P
PAIRS = NB // 2
J = 16
G = 26
T = J * G
EP = T * P
CH = G * P
HALF = G // 2
UNIT = HALF * P
BIG = 3e38
START = 8
EPS = 1e-5


def build(nc, a, out):
    kv_table = nc.dram_tensor("kv_table", (NP, 2 * D), F32, kind="Internal").ap()
    v_edges = nc.dram_tensor("v_edges", (P, T * D), F32, kind="Internal").ap()
    rel_dram = nc.dram_tensor("rel_dram", (G, J * P), BF16, kind="Internal").ap()
    block_dram = nc.dram_tensor("block_dram", (G, J), I32, kind="Internal").ap()

    with ExitStack() as ctx:
        def sb(name, shape, dt=F32):
            return ctx.enter_context(nc.sbuf_tensor(name, shape, dt))

        def sem(name):
            return ctx.enter_context(nc.semaphore(name))

        X = sb("X", [P, NP])
        Y = sb("Y", [P, NP])
        QT = sb("QT", [P, NP + P])
        AG1 = sb("AG1", [P, NP + P])
        AGG = [QT, AG1]
        KV = sb("KV", [P, 2, J, 2 * D])
        OHT = sb("OHT", [P, 2, 2, 8 * P])
        REL = sb("REL", [P, 2, J * P], BF16)
        LB = sb("LB", [P, CH])
        FB = sb("FB", [P, CH + 1])
        MB = sb("MB", [P, CH])
        AE = MB
        ADD_P = sb("ADD_P", [P, CH], BF16)
        ADD_N = sb("ADD_N", [P, CH], BF16)
        SAME_P = sb("SAME_P", [P, CH], U8)
        SAME_N = sb("SAME_N", [P, CH], U8)
        LOOP1 = sb("LOOP1", [P, CH], U8)
        idx = sb("idx", [P, 2, J], U32)
        dst_first = sb("dst_first", [P, T], I32)
        rel_edge = sb("rel_edge", [P, T])
        block_row = sb("block_row", [1, T], I32)
        iota_row = sb("iota_row", [P, P])
        iota_part = sb("iota_part", [P, 2])
        ident = sb("ident", [P, P])
        ones = sb("ones", [1, P])
        Wp = [sb("Wp0", [P, 3 * D]), sb("Wp1", [P, 4 * D])]
        Bp = [sb("Bp0", [1, 3 * D]), sb("Bp1", [1, 4 * D])]
        Wo = sb("Wo", [P, D])
        bo = sb("bo", [1, D])
        We = sb("We", [ED, D])
        W1 = [sb(f"W1{l}", [P, FF]) for l in range(2)]
        W2 = [sb(f"W2{l}", [P, 4, D]) for l in range(2)]
        bf1 = [sb(f"bf1{l}", [P, 4]) for l in range(2)]
        bf2 = [sb(f"bf2{l}", [1, D]) for l in range(2)]
        gb = sb("gb", [P, 4])
        GB = sb("GB", [P, 4, D])
        MEAN = sb("MEAN", [P, NB])
        RS = sb("RS", [P, NB])
        SD = sb("SD", [P, NB])
        BN = sb("BN", [P, NB, 6])
        cols = sb("cols", [P, 4])
        grow = sb("grow", [1, 4, P])
        srow = sb("srow", [1, 2, P + 2])
        TMP = sb("TMP", [P, 1280])

        PS = [ctx.enter_context(nc.psum_tensor(f"PS{b}", [P, 512], F32)) for b in range(8)]

        xn = [TMP[:, k * D:(k + 1) * D] for k in range(2)]
        hN = [TMP[:, 256 + k * D:256 + (k + 1) * D] for k in range(2)]
        hT = TMP[:, 512:768]
        kv_out = [KV[:, 0, k, :] for k in range(2)]
        gT = KV[:, 1, 0:4, :]
        agg_pair = TMP[:, 0:256]
        prod = [TMP[:, r * 512:(r + 1) * 512] for r in range(2)]
        Ls = [TMP[:, 1024 + s * P:1024 + (s + 1) * P] for s in range(2)]
        ea = [AG1[0:ED, hh * 8 * P:(hh + 1) * 8 * P] for hh in range(2)]
        kv_flat = KV[:, :, :, :].rearrange("p s j d -> p (s j d)")
        dstB = kv_flat[:, 0:CH + 2].bitcast(I32)
        srcB = kv_flat[:, CH + 2:2 * CH + 2].bitcast(I32)
        V4 = [kv_flat[:, u * UNIT:(u + 1) * UNIT] for u in range(4)]
        OH4 = [LB[:, 0:UNIT], LB[:, UNIT:2 * UNIT], FB[:, 0:UNIT], FB[:, UNIT:2 * UNIT]]
        dstG = OHT[0:G, 0, :, :].rearrange("p a n -> p (a n)").bitcast(I32)
        relG = REL[0:G, 0, :]
        blkG = OHT[0:G, 1, 0, 0:J].bitcast(I32)
        dst_edge = OHT[:, 1, 1, 0:T].bitcast(I32)

        S = {n: sem(n) for n in """x_loaded dstg_loaded dste_loaded chunks_loaded weights_loaded
            rel_stored block_loaded out_stored""".split()}
        counts = """consts_made rel_made prep_step kv_copied kv_free v_free
            unit_summed0 unit_summed1 unit_summed2 unit_summed3
            gather_begun rel_begun stat_step moment_step var_ready sd_ready rs_ready
            xn_ready tp_ready ht_ready proj_ready q_made x_kept
            ln_affine sum_ready att_ready res_ready hidden_ready gelu_ready ffn_ready ffn_added
            out_made
            oht_ready qe_ready prod_done e_ready e_used l_ready lt_ready lb_ready f_done batch_step
            xc_col xc_row xc_scanned xc_back soft_step shifted exp_ready aet_ready aet_used
            agg_zeroed unit_step sum0_ready sum0_free sum1_ready sum1_free sum1_added act_col
            """.split()
        S.update((n, sem(n)) for n in counts)

        def done(name, n):
            return S[name], n + START

        kv_stored = [sem(f"kv_stored{k}") for k in range(2)]
        idx_loaded = [sem(f"idx_loaded{s}") for s in range(2)]
        rel_loaded = [sem(f"rel_loaded{s}") for s in range(2)]
        ea_loaded = [sem(f"ea_loaded{s}") for s in range(2)]
        gathered = [sem(f"gathered{s}") for s in range(2)]
        v_stored = [sem(f"v_stored{s}") for s in range(2)]
        v_loaded = [sem(f"v_loaded{u}") for u in range(4)]
        pv_ready = [sem(f"pv_ready{u}") for u in range(4)]

        class Steps:

            def __init__(self, eng, name):
                self.eng, self.s, self.base, self.n = eng, S[name], 0, 0
                self.i, self.per = 0, 0

            def loop(self, i, per):
                self.base, self.n, self.i, self.per = self.base + self.n, 0, i, per

            def end(self, trips):
                assert self.n == self.per, (self.n, self.per)
                self.base, self.n, self.i, self.per = self.base + trips * self.per, 0, 0, 0

            def run(self, ins):
                ins.then_inc(self.s, 1)
                self.n += 1
                self.eng.wait_ge(self.s, self.i * self.per + (self.base + self.n + START))

        block = ctx.enter_context(nc.Block())

        @block.sync
        def _(sp):
            sp.dma_start(X[:, :].rearrange("p (b d) -> p b d", b=NB), a["x"].rearrange("(b p) d -> p b d", p=P)).then_inc(S["x_loaded"], 16)
            sp.dma_start(dstG.rearrange("g (j e) -> g j e", j=J),
                         a["dst"][1:EP + 1].rearrange("(j g e) -> g j e", j=J, g=G)).then_inc(S["dstg_loaded"], 16)
            sp.dma_start(dst_edge, a["dst_edge"]).then_inc(S["dste_loaded"], 16)
            sp.dma_start(dst_first[:, :], a["dst_first"].rearrange("(a t) -> a t", a=1).broadcast_to([P, T])).then_inc(S["dste_loaded"], 16)
            for h in range(H):
                sp.dma_start(dstB[h * J:(h + 1) * J, :],
                             bass.AP(a["dst"].tensor, 0, [[CH, J], [1, CH + 2]])).then_inc(S["chunks_loaded"], 16)
                sp.dma_start(srcB[h * J:(h + 1) * J, :],
                             a["src"].rearrange("(j n) -> j n", j=J)).then_inc(S["chunks_loaded"], 16)

            def w(dst, src):
                sp.dma_start(dst, src).then_inc(S["weights_loaded"], 16)

            row = lambda v: v.rearrange("(a n) -> a n", a=1)
            col = lambda v: v.rearrange("(n a) -> n a", a=1)
            for n, q in enumerate(("q", "k", "v")):
                for l in range(2):
                    w(Wp[l][:, n * D:(n + 1) * D], a[f"L{l}_gnn_W{q}"])
                    w(Bp[l][:, n * D:(n + 1) * D], row(a[f"L{l}_gnn_b{q}"]))
            w(Wp[1][:, 3 * D:4 * D], a["L1_gnn_Wskip"])
            w(Bp[1][:, 3 * D:4 * D], row(a["L1_gnn_bskip"]))
            w(Wo[:, :], a["L0_gnn_Wo"])
            w(bo[:, :], row(a["L0_gnn_bo"]))
            w(We[:, :], a["L1_gnn_We"])
            for l, f in ((0, ""), (1, "f")):
                w(W1[l][:, :], a[f"L{l}_gnn_W{f}1"])
                w(W2[l][:, :, :], a[f"L{l}_gnn_W{f}2"].rearrange("(c k) n -> k c n", k=P))
                w(bf2[l][:, :], row(a[f"L{l}_gnn_bf2"]))
                for c in range(4):
                    w(bf1[l][:, c:c + 1], col(a[f"L{l}_gnn_bf1"][c * P:(c + 1) * P]))
            for n, v in enumerate(("g1", "b1", "g2", "b2")):
                w(gb[:, n:n + 1], col(a[f"L0_gnn_{v}"]))
                w(GB[:, n, :], row(a[f"L1_gnn_{v}"]).broadcast_to([P, D]))

            sp.wait_ge(*done("rel_made", 2))
            sp.dma_start(rel_dram, relG).then_inc(S["rel_stored"], 16)
            sp.dma_start(block_dram, blkG).then_inc(S["rel_stored"], 16)
            sp.wait_ge(S["rel_stored"], 32)
            sp.dma_start(block_row[:, :], block_dram.rearrange("g j -> (g j)").rearrange("(a n) -> a n", a=1)).then_inc(S["block_loaded"], 16)

            for l in range(2):
                with sp.Fori(0, PAIRS) as i:
                    for k in range(2):
                        sp.wait_ge(*done("kv_copied", i * 2 + (l * NB + k + 1)))
                        sp.dma_start(kv_table[ds(i * 256 + k * P, P), :], kv_out[k]).then_inc(kv_stored[k], 16)
                    for k in range(2):
                        sp.wait_ge(kv_stored[k], i * 16 + 16 * (PAIRS * l + 1))
                        sp.sem_inc(S["kv_free"], 1)
                with sp.Fori(0, PAIRS) as i:
                    for s in range(2):
                        sp.wait_ge(*done("l_ready", i * 8 + (8 * PAIRS * l + 4 * s - 4)))
                        sp.dma_start(idx[:, s, :], a["src_batch"][ds(i * 2 + s, 1), :, :].rearrange("a p j -> (a p) j")).then_inc(idx_loaded[s], 16)
                        sp.wait_ge(*done("oht_ready", i * 8 + (8 * PAIRS * l + 4 * s - 4)))
                        sp.sem_inc(S["rel_begun"], 1)
                        sp.dma_start(REL[:, s, :], rel_dram[ds(i * 2 + s, 1), :].broadcast_to([P, J * P])).then_inc(rel_loaded[s], 16)
                        if l:
                            for hh in range(2):
                                sp.wait_ge(*done("e_ready", i * 8 + (4 * s + 2 * hh - 2)))
                                sp.dma_start(ea[hh], a["edge_batch"][ds(i * 2 + s, 1), :, hh * 8 * P:(hh + 1) * 8 * P]
                                             .rearrange("a p j -> (a p) j")).then_inc(ea_loaded[hh], 16)
                for s in range(2):
                    sp.wait_ge(v_stored[s], 16 * PAIRS * (l + 1))
                    sp.wait_ge(*done("f_done", NB * (l + 1)))
                with sp.Fori(0, J // 2) as i:
                    for q in range(2):
                        for st in range(2):
                            u = 2 * st + q
                            sp.wait_ge(*done(f"unit_summed{u}", i + l * (J // 2)))
                            sp.dma_start(V4[u], v_edges[:, ds(i * (G * P) + (st * (J // 2) * G + q * HALF) * P, UNIT)]).then_inc(v_loaded[u], 16)
            sp.wait_ge(*done("out_made", NB))
            full = N // P
            sp.dma_start(out[0:full * P, :].rearrange("(b p) d -> p b d", p=P),
                         Y[:, 0:full * P].rearrange("p (b d) -> p b d", b=full)).then_inc(S["out_stored"], 16)
            sp.dma_start(out[full * P:N, :], Y[0:N - full * P, full * P:(full + 1) * P]).then_inc(S["out_stored"], 16)
            sp.wait_ge(S["out_stored"], 32)

        @block.gpsimd
        def _(pool):
            g = nc.gpsimd
            g.memset(ones[:, :], 1.0).then_inc(S["consts_made"], 1)
            g.memset(ident[:, :], 0.0).then_inc(S["consts_made"], 1)
            g.memset(srow[:, :, :], 0.0).then_inc(S["consts_made"], 1)
            g.memset(FB[:, 0:1], -BIG).then_inc(S["consts_made"], 1)
            g.memset(QT[:, NP:NP + P], 0.0).then_inc(S["consts_made"], 1)
            pool.wait_ge(*done("consts_made", 5))
            g.affine_select(out=ident[:, :], in_=ident[:, :], compare_op=ALU.not_equal, fill=1.0,
                            base=0, pattern=[[-1, P]], channel_multiplier=1).then_inc(S["consts_made"], 1)
            g.iota(iota_row[:, :], pattern=[[1, P]], base=0, channel_multiplier=0,
                   allow_small_or_imprecise_dtypes=True).then_inc(S["consts_made"], 1)
            g.iota(iota_part[:, :], pattern=[[P, 2]], base=0, channel_multiplier=1,
                   allow_small_or_imprecise_dtypes=True).then_inc(S["consts_made"], 1)

            pool.wait_ge(S["weights_loaded"], 16 * WEIGHTS)
            for l in range(2):
                if l:
                    with pool.Fori(0, PAIRS) as i:
                        for k in range(2):
                            pool.wait_ge(*done("xn_ready", i * 2 + (2 * NB + k + 1)))
                            g.tensor_copy(X[:, ds(i * 256 + k * P, P)], xn[k]).then_inc(S["x_kept"], 1)
                for k in range(2):
                    pool.wait_ge(kv_stored[k], 16 * PAIRS * (l + 1))
                pool.wait_ge(*done("prep_step", 8))
                with pool.Fori(0, PAIRS) as i:
                    for s in range(2):
                        pool.wait_ge(idx_loaded[s], i * 16 + 16 * (PAIRS * l + 1))
                        pool.wait_ge(*done("l_ready", i * 8 + (8 * PAIRS * l + 4 * s - 4)))
                        pool.wait_ge(*done("v_free", i * 2 + (NB * l + s - 1)))
                        pool.sem_inc(S["gather_begun"], 1)
                        for j in range(J):
                            g.indirect_dma_start(KV[:, s, j, :], None, kv_table,
                                                 bass.IndirectOffsetOnAxis(ap=idx[:, s, j:j + 1], axis=0)).then_inc(gathered[s], 16)
                pool.wait_ge(*done("f_done", NB * (l + 1)))
                for st in range(2):
                    g.memset(AGG[st][:, :], 0.0).then_inc(S["agg_zeroed"], 1)
                if l:
                    with pool.Fori(0, PAIRS) as i:
                        for k in range(2):
                            pool.wait_ge(*done("xn_ready", i * 2 + (3 * NB + k + 1)))
                            pool.wait_ge(*done("ffn_added", i * 2 + 2 * PAIRS))
                            g.tensor_tensor(hN[k], xn[k], GB[:, 0, :], ALU.mult).then_inc(S["ln_affine"], 1)
                            pool.wait_ge(*done("ln_affine", i * 4 + (2 * k + 1)))
                            g.tensor_tensor(hN[k], hN[k], GB[:, 1, :], ALU.add).then_inc(S["ln_affine"], 1)
                    with pool.Fori(0, PAIRS) as i:
                        for k in range(2):
                            pool.wait_ge(*done("xn_ready", i * 2 + (4 * NB + k + 1)))
                            g.tensor_tensor(hN[k], xn[k], GB[:, 2, :], ALU.mult).then_inc(S["ln_affine"], 1)
                            pool.wait_ge(*done("ln_affine", i * 4 + (4 * PAIRS + 2 * k + 1)))
                            g.tensor_tensor(hN[k], hN[k], GB[:, 3, :], ALU.add).then_inc(S["ln_affine"], 1)

        @block.scalar
        def _(act):
            sc = nc.scalar

            def roots(n):
                act.wait_ge(*done("var_ready", n))
                sc.activation(SD[:, :], RS[:, :], ACT.Sqrt).then_inc(S["sd_ready"], 1)

            act.sem_inc(S["sum0_free"], 4)
            act.wait_ge(S["weights_loaded"], 16 * WEIGHTS)
            for l in range(2):
                if l == 0:
                    roots(1)
                if l == 0:
                    act.wait_ge(*done("prep_step", 8))
                with act.Fori(0, PAIRS) as i:
                    act.wait_ge(*done("tp_ready", i + (2 * PAIRS * l + 1)))
                    if l == 0:
                        sc.activation(hT, PS[0][:, 0:256], ACT.Identity, bias=gb[:, 1:2], scale=gb[:, 0:1]).then_inc(S["ht_ready"], 1)
                    else:
                        sc.activation(hT, PS[0][:, 0:256], ACT.Copy).then_inc(S["ht_ready"], 1)
                    for k in range(2):
                        act.wait_ge(*done("q_made", i * 2 + (NB * l + k + 1)))
                        act.wait_ge(*done("kv_free", i * 2 + (NB * l + k - 1)))
                        sc.activation(kv_out[k], PS[1 + k][:, D:3 * D], ACT.Copy).then_inc(S["kv_copied"], 1)
                with act.Fori(0, PAIRS) as i:
                    for s in range(2):
                        if l == 0:
                            act.wait_ge(gathered[s], i * 256 + 256)
                        else:
                            act.wait_ge(*done("e_used", i * 8 + 4 * s + 4))
                        act.dma_start(v_edges.rearrange("p (j n) -> p j n", j=J)[:, :, ds(i * 256 + s * P, P)],
                                      KV[:, s, :, D:2 * D]).then_inc(v_stored[s], 16)
                        act.wait_ge(*done("lt_ready", i * 2 + (NB * l + s + 1)))
                        sc.activation(LB[:, ds(i * 256 + s * P, P)], PS[6][:, s * P:(s + 1) * P], ACT.Copy).then_inc(S["lb_ready"], 1)
                        act.wait_ge(v_stored[s], i * 16 + 16 * (PAIRS * l + 1))
                        act.sem_inc(S["v_free"], 1)
                act.wait_ge(*done("shifted", l + 1))
                sc.activation(LB[:, :], LB[:, :], ACT.Exp).then_inc(S["exp_ready"], 1)
                for b in range(0, G, 4):
                    act.wait_ge(*done("aet_ready", 7 * l + b // 4 + 1))
                    w_ = min(4, G - b) * P
                    sc.activation(AE[:, b * P:b * P + w_], PS[b // 4 % 4][:, 0:w_], ACT.Copy).then_inc(S["aet_used"], 1)
                act.wait_ge(*done("agg_zeroed", 2 * (l + 1)))
                with act.Fori(0, J // 2) as i:
                    for q in range(2):
                        for m in range(HALF):
                            n = q * HALF + m
                            if m % 4 == 0:
                                act.wait_ge(*done("sum0_ready", i * 8 + (l * 64 + q * 4 + m // 4 + 1)))
                            first = act.value_load(dst_first[0:1, ds(i * G + n, 1)], min_val=0, max_val=N)
                            p = PS[m // 4][:, m % 4 * P:(m % 4 + 1) * P]
                            act.wait_ge(*done("act_col", i * (2 * G) + (l * 16 * G + 2 * n)))
                            sc.activation(QT[:, ds(first, 1)], p[:, 0:1], ACT.Identity, bias=QT[:, ds(first, 1)]).then_inc(S["act_col"], 1)
                            sc.activation(QT[:, ds(first + 1, P - 1)], p[:, 1:P], ACT.Copy).then_inc(S["act_col"], 1)
                            if m % 4 == 3 or m == HALF - 1:
                                act.wait_ge(*done("act_col", i * (2 * G) + (l * 16 * G + 2 * n + 2)))
                                act.sem_inc(S["sum0_free"], 1)
                roots(2 if l == 0 else 4)
                with act.Fori(0, PAIRS) as i:
                    act.wait_ge(*done("tp_ready", i + (PAIRS * (2 * l + 1) + 1)))
                    if l == 0:
                        sc.activation(hT, PS[0][:, 0:256], ACT.Identity, bias=gb[:, 3:4], scale=gb[:, 2:3]).then_inc(S["ht_ready"], 1)
                    else:
                        sc.activation(hT, PS[0][:, 0:256], ACT.Copy).then_inc(S["ht_ready"], 1)
                    for c in range(4):
                        if c % 2 == 0:
                            act.wait_ge(*done("hidden_ready", i * 2 + (2 * PAIRS * l + c // 2 + 1)))
                        sc.activation(gT[:, c, :], PS[1 + c // 2][:, c % 2 * 256:(c % 2 + 1) * 256], ACT.Gelu,
                                      bias=bf1[l][:, c:c + 1]).then_inc(S["gelu_ready"], 1)
                roots(3 if l == 0 else 5)
            roots(6)

        @block.tensor
        def _(pe):
            te = nc.tensor
            for n in counts:
                pe.sem_inc(S[n], START)
            xc = [0]

            def exchange(col, part):
                xc[0] += 1
                pe.wait_ge(*done("xc_col", xc[0]))
                te.matmul(PS[7][0:1, 0:P], col, ident[:, :], start=True, stop=True).then_inc(S["xc_row"], 1)
                pe.wait_ge(*done("xc_scanned", xc[0]))
                te.matmul(PS[7][:, P:P + 1], part, ones[0:1, 0:1], start=True, stop=True).then_inc(S["xc_back"], 1)

            fwd, bwd = srow[0:1, 0, 0:P], srow[0:1, 1, 1:P + 1]

            pe.wait_ge(*done("consts_made", 8))
            pe.wait_ge(*done("prep_step", 6))
            te.matmul(PS[7][0:1, 0:P], cols[:, 0:1], ident[:, :], start=True, stop=True)
            te.matmul(PS[7][0:1, P:2 * P], cols[:, 1:2], ident[:, :], start=True, stop=True).then_inc(S["xc_row"], 1)
            exchange(FB[:, CH:CH + 1], fwd)
            pe.wait_ge(S["weights_loaded"], 16 * WEIGHTS)

            def turn(src, base):
                def body(i):
                    for k in range(2):
                        if src is xn:
                            pe.wait_ge(*done("xn_ready", i * 2 + (base[0] + k + 1)))
                        else:
                            pe.wait_ge(*done("ln_affine", i * 4 + (2 * k + 2)))
                        last = te.transpose(PS[0][:, k * P:(k + 1) * P], src[k], ident[:, :])
                    last.then_inc(S["tp_ready"], 1)
                return body

            for l in range(2):
                Wd = (3 + l) * D
                t = turn(xn, [2 * NB * l])
                with pe.Fori(0, PAIRS) as i:
                    t(i)
                    pe.wait_ge(*done("ht_ready", i + (2 * PAIRS * l + 1)))
                    for k in range(2):
                        pe.wait_ge(*done("kv_copied", i * 2 + (NB * l + k - 1)))
                        te.matmul(PS[1 + k][:, 0:Wd], ones[:, :], Bp[l][:, :], start=True, stop=False)
                        te.matmul(PS[1 + k][:, 0:Wd], hT[:, k * P:(k + 1) * P], Wp[l][:, :], start=False, stop=True).then_inc(S["proj_ready"], 1)
                pe.wait_ge(S["block_loaded"], 16)
                pe.wait_ge(*done("q_made", NB * (l + 1)))
                pe.wait_ge(*done("kv_copied", NB * (l + 1)))
                with pe.Fori(0, PAIRS) as i:
                    for s in range(2):
                        for q4 in range(4):
                            hh = q4 // 2
                            if q4 % 2 == 0:
                                pe.wait_ge(*done("oht_ready", i * 8 + (8 * PAIRS * l + 4 * s + 2 * hh + 2)))
                                if l:
                                    pe.wait_ge(ea_loaded[hh], i * 32 + 16 * (s + 1))
                            pe.wait_ge(*done("prod_done", i * 8 + (8 * PAIRS * l + 4 * s + q4 - 3)))
                            for jj in range(4):
                                j = 4 * q4 + jj
                                blk = pe.value_load(block_row[0:1, ds(i * 2 * J + s * J + j, 1)], min_val=0, max_val=NP - P)
                                o = PS[q4][:, jj * P:(jj + 1) * P]
                                e0 = (j % 8) * P
                                te.matmul(o, OHT[:, hh, 0, e0:e0 + P], QT[:, ds(blk, P)], start=True, stop=False)
                                last = te.matmul(o, OHT[:, hh, 1, e0:e0 + P], QT[:, ds(blk + P, P)], start=False, stop=True)
                            last.then_inc(S["qe_ready"], 1)
                            if l:
                                pe.wait_ge(*done("e_used", i * 8 + (4 * s + q4 - 1)))
                                for jj in range(4):
                                    e0 = ((4 * q4 + jj) % 8) * P
                                    last = te.matmul(PS[4 + q4 % 2][:, jj * P:(jj + 1) * P], ea[hh][:, e0:e0 + P], We[:, :], start=True, stop=True)
                                last.then_inc(S["e_ready"], 1)
                        pe.wait_ge(*done("l_ready", i * 8 + (8 * PAIRS * l + 4 * s + 4)))
                        pe.wait_ge(*done("lb_ready", i * 2 + (NB * l + s)))
                        te.transpose(PS[6][:, s * P:(s + 1) * P], Ls[s], ident[:, :]).then_inc(S["lt_ready"], 1)
                exchange(FB[:, CH:CH + 1], fwd)
                exchange(MB[:, 0:1], bwd)
                exchange(FB[:, CH:CH + 1], fwd)
                exchange(MB[:, 0:1], bwd)
                pe.wait_ge(*done("soft_step", SOFT * (l + 1)))
                for b in range(0, G, 4):
                    if b >= 16:
                        pe.wait_ge(*done("aet_used", 7 * l + b // 4 - 3))
                    for n in range(b, min(b + 4, G)):
                        last = te.transpose(PS[b // 4 % 4][:, (n - b) * P:(n - b + 1) * P], LB[:, n * P:(n + 1) * P], ident[:, :])
                    last.then_inc(S["aet_ready"], 1)
                pe.wait_ge(*done("aet_used", 7 * (l + 1)))
                with pe.Fori(0, J // 2) as i:
                    for q in range(2):
                        for st in range(2):
                            pe.wait_ge(pv_ready[2 * st + q], i * 2 + (l * J + 2))
                        for b in range(4):
                            for st in range(2):
                                u = 2 * st + q
                                pe.wait_ge(*done(f"sum{st}_free", i * 8 + (l * 64 + q * 4 + b + 1)))
                                for m in range(4 * b, min(4 * b + 4, HALF)):
                                    last = te.matmul(PS[4 * st + b][:, m % 4 * P:(m % 4 + 1) * P],
                                                     V4[u][:, m * P:(m + 1) * P], OH4[u][:, m * P:(m + 1) * P], start=True, stop=True)
                                last.then_inc(S[f"sum{st}_ready"], 1)
                        for st in range(2):
                            pe.wait_ge(*done(f"sum{st}_ready", i * 8 + (l * 64 + q * 4 + 4)))
                            pe.sem_inc(S[f"unit_summed{2 * st + q}"], 1)
                for st in range(2):
                    pe.wait_ge(*done(f"sum{st}_free", 64 * (l + 1) + 4))
                with pe.Fori(0, PAIRS) as i:
                    pe.wait_ge(*done("sum_ready", i + (PAIRS * l + 1)))
                    pe.wait_ge(*done("res_ready", i + PAIRS * l))
                    for k in range(2):
                        o = PS[0][:, k * P:(k + 1) * P]
                        lhs = agg_pair[:, k * P:(k + 1) * P]
                        if l == 0:
                            te.matmul(o, ones[:, :], bo[:, :], start=True, stop=False)
                            last = te.matmul(o, lhs, Wo[:, :], start=False, stop=True)
                        else:
                            last = te.transpose(o, lhs, ident[:, :])
                    last.then_inc(S["att_ready"], 1)
                pe.wait_ge(*done("res_ready", PAIRS * (l + 1)))
                t = turn(xn if l == 0 else hN, [NB])
                with pe.Fori(0, PAIRS) as i:
                    t(i)
                    pe.wait_ge(*done("ht_ready", i + (PAIRS * (2 * l + 1) + 1)))
                    pe.wait_ge(*done("gelu_ready", i * 4 + 4 * PAIRS * l))
                    for c in range(4):
                        last = te.matmul(PS[1 + c // 2][:, c % 2 * 256:(c % 2 + 1) * 256], W1[l][:, c * P:(c + 1) * P], hT, start=True, stop=True)
                        if c % 2:
                            last.then_inc(S["hidden_ready"], 1)
                    pe.wait_ge(*done("gelu_ready", i * 4 + (4 * PAIRS * l + 4)))
                    pe.wait_ge(*done("ffn_added", i * 2 + 2 * PAIRS * l))
                    for k in range(2):
                        o = PS[3][:, k * P:(k + 1) * P]
                        te.matmul(o, ones[:, :], bf2[l][:, :], start=True, stop=False)
                        for c in range(4):
                            last = te.matmul(o, gT[:, c, k * P:(k + 1) * P], W2[l][:, c, :], start=False, stop=(c == 3))
                    last.then_inc(S["ffn_ready"], 1)
                pe.wait_ge(*done("ffn_added", 2 * PAIRS * (l + 1)))

        @block.vector
        def _(dve):
            v = nc.vector
            prep = Steps(dve, "prep_step")
            stat = Steps(dve, "stat_step")
            xc = [0]

            def scan(o, gate, data, init, op0, op1):
                return v.tensor_tensor_scan(o, gate, data, init, op0, op1)

            def exchange(forward, gate, op0, op1):
                xc[0] += 1
                dve.wait_ge(*done("xc_row", xc[0] + 1))
                if forward:
                    scan(srow[0:1, 0, 1:P + 1], grow[0:1, gate, :], PS[7][0:1, 0:P], 0.0, op0, op1).then_inc(S["xc_scanned"], 1)
                else:
                    scan(srow[0:1, 1, 0:P][:, ::-1], grow[0:1, gate, ::-1], PS[7][0:1, 0:P][:, ::-1], 0.0, op0, op1).then_inc(S["xc_scanned"], 1)
                dve.wait_ge(*done("xc_back", xc[0]))
                return v.tensor_copy(cols[:, 2:3], PS[7][:, P:P + 1])

            def block_stats(src, k, i):
                dve.wait_ge(S["x_loaded"], 16)
                v.bn_stats(BN[:, ds(i * 2 + k, 1), :].rearrange("p a c -> p (a c)"), src).then_inc(S["stat_step"], 1)
                stat.n += 1

            def inv_std(n):
                dve.wait_ge(*done("stat_step", stat.base))
                even, odd = BN[:, :, 1], BN[:, :, 4]
                v.tensor_tensor(MEAN[:, :], even, odd, ALU.add).then_inc(S["moment_step"], 1)
                v.tensor_tensor(SD[:, :], even, odd, ALU.subtract).then_inc(S["moment_step"], 1)
                v.tensor_tensor(RS[:, :], BN[:, :, 2], BN[:, :, 5], ALU.add).then_inc(S["moment_step"], 1)
                dve.wait_ge(*done("moment_step", 7 * n - 4))
                v.tensor_scalar(MEAN[:, :], MEAN[:, :], 0.5, None, ALU.mult).then_inc(S["moment_step"], 1)
                v.scalar_tensor_tensor(SD[:, :], SD[:, :], 0.25, SD[:, :], ALU.mult, ALU.mult).then_inc(S["moment_step"], 1)
                v.tensor_scalar(RS[:, :], RS[:, :], 1.0 / D, EPS, ALU.mult, ALU.add).then_inc(S["moment_step"], 1)
                dve.wait_ge(*done("moment_step", 7 * n - 1))
                v.tensor_tensor(RS[:, :], RS[:, :], SD[:, :], ALU.add).then_inc(S["moment_step"], 1)
                dve.wait_ge(*done("moment_step", 7 * n))
                dve.sem_inc(S["var_ready"], 1)
                dve.wait_ge(*done("sd_ready", n))
                v.reciprocal(RS[:, :], SD[:, :]).then_inc(S["rs_ready"], 1)
                dve.wait_ge(*done("rs_ready", n))

            def normalise(o, src, i, k):
                return v.tensor_scalar(o, src[:, ds(i * 256 + k * P, P)], MEAN[:, ds(i * 2 + k, 1)], RS[:, ds(i * 2 + k, 1)],
                                       ALU.subtract, ALU.mult)

            dve.sem_inc(S["sum1_free"], 4)
            dve.wait_ge(S["dstg_loaded"], 16)
            g3 = dstG.rearrange("g (j e) -> g j e", j=J)
            v.tensor_scalar(blkG, g3[:, :, 0], 7, 7, ALU.logical_shift_right, ALU.logical_shift_left).then_inc(S["rel_made"], 1)
            dve.wait_ge(*done("rel_made", 1))
            v.tensor_tensor(relG.rearrange("g (j e) -> g j e", j=J), g3, blkG.unsqueeze(2).broadcast_to([G, J, P]), ALU.subtract)\
                .then_inc(S["rel_made"], 1)
            dve.wait_ge(S["dste_loaded"], 32)
            prep.run(v.tensor_tensor(rel_edge[:, :], dst_edge, dst_first[:, :], ALU.subtract))
            dve.wait_ge(S["chunks_loaded"], 16 * 2 * H)
            here = dstB[:, 1:CH + 1]
            prep.run(v.tensor_tensor(SAME_P[:, :], dstB[:, 0:CH], here, ALU.is_equal))
            prep.run(v.tensor_tensor(SAME_N[:, :], here, dstB[:, 2:CH + 2], ALU.is_equal))
            prep.run(v.tensor_reduce(cols[:, 0:1], SAME_P[:, :], AX.X, ALU.min))
            prep.run(v.tensor_reduce(cols[:, 1:2], SAME_N[:, :], AX.X, ALU.min))
            prep.run(v.tensor_scalar(ADD_P[:, :], SAME_P[:, :], 1.0, BIG, ALU.subtract, ALU.mult))
            prep.run(v.tensor_scalar(ADD_N[:, :], SAME_N[:, :], 1.0, BIG, ALU.subtract, ALU.mult))
            prep.run(v.tensor_tensor(LB[:, :], srcB, here, ALU.is_equal))
            dve.wait_ge(*done("xc_row", 1))
            prep.run(v.tensor_copy(grow[:, 0:2, :].rearrange("a b n -> a (b n)"), PS[7][0:1, 0:2 * P]))
            prep.run(v.tensor_scalar(grow[:, 2:4, :], grow[:, 0:2, :], 1.0, BIG, ALU.subtract, ALU.mult))
            dve.wait_ge(*done("consts_made", 8))
            scan(FB[:, 1:CH + 1], SAME_P[:, :], LB[:, :], 0.0, ALU.mult, ALU.add).then_inc(S["xc_col"], 1)
            prep.run(exchange(True, 0, ALU.mult, ALU.add))
            prep.run(scan(FB[:, 1:CH + 1], SAME_P[:, :], LB[:, :], cols[:, 2:3], ALU.mult, ALU.add))
            prep.run(v.scalar_tensor_tensor(LOOP1[:, :], FB[:, 1:CH + 1], 1.0, LB[:, :], ALU.is_equal, ALU.mult))
            dve.wait_ge(S["x_loaded"], 16)
            with dve.Fori(0, PAIRS) as i:
                stat.loop(i, 2)
                for k in range(2):
                    block_stats(X[:, ds(i * 256 + k * P, P)], k, i)
            stat.end(PAIRS)
            inv_std(1)
            dve.wait_ge(S["weights_loaded"], 16 * WEIGHTS)

            for l in range(2):
                soft = Steps(dve, "soft_step")
                soft.base = SOFT * l
                with dve.Fori(0, PAIRS) as i:
                    for k in range(2):
                        if l:
                            dve.wait_ge(*done("x_kept", i * 2))
                            dve.wait_ge(*done("batch_step", i * 2))
                        normalise(xn[k], X, i, k).then_inc(S["xn_ready"], 1)
                    for k in range(2):
                        dve.wait_ge(*done("proj_ready", i * 2 + (NB * l + k + 1)))
                        at = ds(i * 256 + k * P, P)
                        if l:
                            v.tensor_tensor(Y[:, at], PS[1 + k][:, 3 * D:4 * D], xn[k], ALU.add).then_inc(S["batch_step"], 1)
                        v.tensor_scalar(QT[:, at], PS[1 + k][:, 0:D], 0.25, None, ALU.mult).then_inc(S["q_made"], 1)
                if l:
                    dve.wait_ge(*done("batch_step", NB))
                    dve.wait_ge(*done("x_kept", NB))
                dve.wait_ge(S["rel_stored"], 32)
                with dve.Fori(0, PAIRS) as i:
                    for s in range(2):
                        g0 = i * 256 + s * P
                        dve.wait_ge(rel_loaded[s], i * 16 + 16 * (PAIRS * l + 1))
                        for hh in range(2):
                            dve.wait_ge(*done("qe_ready", i * 8 + (8 * PAIRS * l + 4 * s + 2 * hh - 2)))
                            for nf in range(2):
                                v.tensor_scalar(OHT[:, hh, nf, :], REL[:, s, hh * 8 * P:(hh + 1) * 8 * P], iota_part[:, nf:nf + 1], None,
                                                ALU.is_equal).then_inc(S["oht_ready"], 1)
                        dve.wait_ge(gathered[s], i * 256 + 256 * (PAIRS * l + 1))
                        for q4 in range(4):
                            kk = KV[:, s, 4 * q4:4 * q4 + 4, 0:D]
                            if l:
                                dve.wait_ge(*done("e_ready", i * 8 + (4 * s + q4 + 1)))
                                ep = PS[4 + q4 % 2][:, :].rearrange("p (j d) -> p j d", j=4)
                                vv = KV[:, s, 4 * q4:4 * q4 + 4, D:2 * D]
                                v.tensor_tensor(kk, kk, ep, ALU.add).then_inc(S["batch_step"], 1)
                                v.tensor_tensor(vv, vv, ep, ALU.add).then_inc(S["e_used"], 1)
                                dve.wait_ge(*done("batch_step", i * 8 + (NB + 4 * s + q4 + 1)))
                            dve.wait_ge(*done("qe_ready", i * 8 + (8 * PAIRS * l + 4 * s + q4 + 1)))
                            pr = prod[q4 % 2]
                            v.tensor_tensor(pr.rearrange("p (j d) -> p j d", j=4), kk, PS[q4][:, :].rearrange("p (j d) -> p j d", j=4),
                                            ALU.mult).then_inc(S["prod_done"], 1)
                            dve.wait_ge(*done("prod_done", i * 8 + (8 * PAIRS * l + 4 * s + q4 + 1)))
                            if q4 == 0:
                                dve.wait_ge(*done("lt_ready", i * 2 + (NB * l + s - 1)))
                            v.tensor_reduce(Ls[s].rearrange("p (h j) -> p j h", h=H)[:, 4 * q4:4 * q4 + 4, :],
                                            pr.rearrange("p (j h c) -> p j h c", j=4, h=H), AX.X, ALU.add).then_inc(S["l_ready"], 1)
                        dve.wait_ge(*done("lb_ready", i * 2 + (NB * l + s + 1)))
                        dve.wait_ge(*done("f_done", i * 2 + NB * l + (1 if s else 0)))
                        scan(FB[:, ds(g0 + 1, P)], ADD_P[:, ds(g0, P)], LB[:, ds(g0, P)], FB[:, ds(g0, 1)], ALU.add, ALU.max).then_inc(S["f_done"], 1)
                dve.wait_ge(*done("f_done", NB * (l + 1)))
                dve.sem_inc(S["xc_col"], 1)
                F1 = FB[:, 1:CH + 1]
                rev = lambda x: x[:, ::-1]
                soft.run(exchange(True, 2, ALU.add, ALU.max))
                soft.run(scan(F1, ADD_P[:, :], LB[:, :], cols[:, 2:3], ALU.add, ALU.max))
                scan(rev(MB[:, :]), rev(ADD_N[:, :]), rev(F1), -BIG, ALU.add, ALU.max).then_inc(S["xc_col"], 1)
                soft.run(exchange(False, 3, ALU.add, ALU.max))
                soft.run(scan(rev(MB[:, :]), rev(ADD_N[:, :]), rev(F1), cols[:, 2:3], ALU.add, ALU.max))
                v.tensor_tensor(LB[:, :], LB[:, :], MB[:, :], ALU.subtract).then_inc(S["shifted"], 1)
                dve.wait_ge(*done("exp_ready", l + 1))
                if l == 0:
                    soft.run(v.scalar_tensor_tensor(LB[:, :], LOOP1[:, :], 1.0, LB[:, :], ALU.add, ALU.mult))
                else:
                    dve.sem_inc(S["soft_step"], 1)
                    soft.n += 1
                scan(F1, SAME_P[:, :], LB[:, :], 0.0, ALU.mult, ALU.add).then_inc(S["xc_col"], 1)
                soft.run(exchange(True, 0, ALU.mult, ALU.add))
                soft.run(scan(F1, SAME_P[:, :], LB[:, :], cols[:, 2:3], ALU.mult, ALU.add))
                scan(rev(MB[:, :]), rev(SAME_N[:, :]), rev(F1), 0.0, ALU.mult, ALU.max).then_inc(S["xc_col"], 1)
                soft.run(exchange(False, 1, ALU.mult, ALU.max))
                soft.run(scan(rev(MB[:, :]), rev(SAME_N[:, :]), rev(F1), cols[:, 2:3], ALU.mult, ALU.max))
                soft.run(v.reciprocal(MB[:, :], MB[:, :]))
                soft.run(v.tensor_tensor(LB[:, :], LB[:, :], MB[:, :], ALU.mult))
                assert soft.n == SOFT
                dve.wait_ge(*done("aet_used", 7 * (l + 1)))
                dve.wait_ge(*done("agg_zeroed", 2 * (l + 1)))
                ae4 = AE[:, :].rearrange("p (g h j) -> p g h j", g=G, h=H)
                with dve.Fori(0, J // 2) as i:
                    for q in range(2):
                        for st in range(2):
                            u = 2 * st + q
                            dve.wait_ge(*done(f"unit_summed{u}", i + l * (J // 2)))
                            v.tensor_tensor(OH4[u].rearrange("p (m n) -> p m n", m=HALF),
                                            iota_row[:, :].unsqueeze(1).broadcast_to([P, HALF, P]),
                                            rel_edge[:, ds(i * G + (st * 8 * G + q * HALF), HALF)].unsqueeze(2).broadcast_to([P, HALF, P]),
                                            ALU.is_equal).then_inc(pv_ready[u], 1)
                            dve.wait_ge(v_loaded[u], i * 16 + 16 * (l * 8 + 1))
                            v4 = V4[u].rearrange("p (m h c) -> p m h c", m=HALF, h=H)
                            at = ae4[:, q * HALF:(q + 1) * HALF, :, ds(i + 8 * st, 1)].broadcast_to([P, HALF, H, C])
                            v.tensor_tensor(v4, v4, at, ALU.mult).then_inc(pv_ready[u], 1)
                        for m in range(HALF):
                            n = q * HALF + m
                            first = dve.value_load(dst_first[0:1, ds(i * G + 8 * G + n, 1)], min_val=0, max_val=N)
                            if m % 4 == 0:
                                dve.wait_ge(*done("sum1_ready", i * 8 + (l * 64 + q * 4 + m // 4 + 1)))
                            dve.wait_ge(*done("sum1_added", i * G + (l * 8 * G + n)))
                            at = AG1[:, ds(first, P)]
                            v.tensor_tensor(at, at, PS[4 + m // 4][:, m % 4 * P:(m % 4 + 1) * P], ALU.add).then_inc(S["sum1_added"], 1)
                            if m % 4 == 3 or m == HALF - 1:
                                dve.wait_ge(*done("sum1_added", i * G + (l * 8 * G + n + 1)))
                                dve.sem_inc(S["sum1_free"], 1)
                for st in range(2):
                    dve.wait_ge(*done(f"sum{st}_free", 64 * (l + 1) + 4))
                with dve.Fori(0, PAIRS) as i:
                    at = ds(i * 256, 256)
                    dve.wait_ge(*done("att_ready", i + PAIRS * l))
                    v.tensor_tensor(agg_pair, QT[:, at], AG1[:, at], ALU.add).then_inc(S["sum_ready"], 1)
                    dve.wait_ge(*done("att_ready", i + (PAIRS * l + 1)))
                    v.tensor_tensor(Y[:, at], PS[0][:, 0:256], (Y if l else X)[:, at], ALU.add).then_inc(S["res_ready"], 1)
                    dve.wait_ge(*done("res_ready", i + (PAIRS * l + 1)))
                    stat.loop(i, 2)
                    for k in range(2):
                        block_stats(Y[:, ds(i * 256 + k * P, P)], k, i)
                    stat.end(PAIRS)
                inv_std(2 if l == 0 else 4)
                with dve.Fori(0, PAIRS) as i:
                    for k in range(2):
                        normalise(xn[k], Y, i, k).then_inc(S["xn_ready"], 1)
                    at = ds(i * 256, 256)
                    dve.wait_ge(*done("ffn_ready", i + (PAIRS * l + 1)))
                    if l == 0:
                        v.tensor_tensor(Y[:, at], PS[3][:, 0:256], Y[:, at], ALU.add).then_inc(S["ffn_added"], 1)
                        dve.wait_ge(*done("ffn_added", i * 2 + 1))
                        v.tensor_tensor(X[:, at], X[:, at], Y[:, at], ALU.add).then_inc(S["ffn_added"], 1)
                        dve.wait_ge(*done("ffn_added", i * 2 + 2))
                    else:
                        v.tensor_tensor(Y[:, at], PS[3][:, 0:256], TMP[:, 256:512], ALU.add).then_inc(S["ffn_added"], 2)
                        dve.wait_ge(*done("ffn_added", i * 2 + (2 * PAIRS + 2)))
                    stat.loop(i, 2)
                    for k in range(2):
                        block_stats((Y if l else X)[:, ds(i * 256 + k * P, P)], k, i)
                    stat.end(PAIRS)
                inv_std(3 if l == 0 else 5)
            with dve.Fori(0, PAIRS) as i:
                for k in range(2):
                    normalise(xn[k], Y, i, k).then_inc(S["xn_ready"], 1)
                at = ds(i * 256, 256)
                dve.wait_ge(*done("ln_affine", i * 4 + (4 * PAIRS + 4)))
                v.tensor_tensor(X[:, at], X[:, at], TMP[:, 256:512], ALU.add).then_inc(S["batch_step"], 1)
                dve.wait_ge(*done("batch_step", i + (NB + 8 * PAIRS + 1)))
                stat.loop(i, 2)
                for k in range(2):
                    block_stats(X[:, ds(i * 256 + k * P, P)], k, i)
                stat.end(PAIRS)
            inv_std(6)
            with dve.Fori(0, PAIRS) as i:
                for k in range(2):
                    normalise(Y[:, ds(i * 256 + k * P, P)], X, i, k).then_inc(S["out_made"], 1)


SOFT = 11
WEIGHTS = 39

_SHAPED = ["L0_gnn_Wq", "L0_gnn_bq", "L0_gnn_Wk", "L0_gnn_bk", "L0_gnn_Wv", "L0_gnn_bv", "L0_gnn_Wo", "L0_gnn_bo",
           "L0_gnn_g1", "L0_gnn_b1", "L0_gnn_g2", "L0_gnn_b2", "L0_gnn_W1", "L0_gnn_bf1", "L0_gnn_W2", "L0_gnn_bf2",
           "L1_gnn_Wq", "L1_gnn_bq", "L1_gnn_Wk", "L1_gnn_bk", "L1_gnn_Wv", "L1_gnn_bv", "L1_gnn_We", "L1_gnn_Wskip",
           "L1_gnn_bskip", "L1_gnn_g1", "L1_gnn_b1", "L1_gnn_g2", "L1_gnn_b2", "L1_gnn_Wf1", "L1_gnn_bf1",
           "L1_gnn_Wf2", "L1_gnn_bf2"]


def kernel(**inputs):
    import numpy as np
    import concourse.bacc as bacc
    from concourse.bass_utils import run_bass_kernel_spmd as run

    nc = bacc.Bacc("TRN2", target_bir_lowering=False, num_devices=1)
    src = np.zeros(EP, np.int32)
    src[:E] = inputs["src"]
    dst = np.full(EP + 2, N, np.int32)
    dst[0] = -1
    dst[EP + 1] = N + 1
    dst[1:E + 1] = inputs["dst"]
    x = np.zeros((NP, D), np.float32)
    x[:N] = inputs["x"]
    edges = np.zeros((EP, ED), np.float32)
    edges[:E] = inputs["edge_attr_64"]
    arrays = {
        "x": x,
        "src": src,
        "dst": dst,
        "src_batch": np.ascontiguousarray(src.reshape(J, G, P).transpose(1, 2, 0)),
        "dst_edge": np.ascontiguousarray(dst[1:EP + 1].reshape(T, P).T),
        "dst_first": np.ascontiguousarray(dst[1:EP + 1].reshape(T, P)[:, 0]),
        "edge_batch": np.ascontiguousarray(edges.reshape(J, G, P, ED).transpose(1, 3, 0, 2)).reshape(G, ED, J * P),
    }
    for name in _SHAPED:
        arrays[name] = np.ascontiguousarray(inputs[name])
    a = {}
    for name, v in arrays.items():
        dt = U32 if name == "src_batch" else mybir.dt.from_np(v.dtype)
        a[name] = nc.dram_tensor(f"in_{name}", v.shape, dt, kind="ExternalInput").ap()
    out = nc.dram_tensor("out_0", (N, D), F32, kind="ExternalOutput").ap()
    build(nc, a, out)
    r = run(nc, [{f"in_{k}": v for k, v in arrays.items()}], core_ids=[0])
    return r.results[0]["out_0"]
```

```python
from contextlib import ExitStack

import concourse.bass as bass
from concourse import mybir

F32 = mybir.dt.float32
BF16 = mybir.dt.bfloat16
I32 = mybir.dt.int32
U32 = mybir.dt.uint32
U8 = mybir.dt.uint8
ACT = mybir.ActivationFunctionType
ALU = mybir.AluOpType
AX = mybir.AxisListType
ENG = mybir.EngineType
ds = bass.ds

P = 128
N = 3125
E = 53125
D = 128
H = 8
C = D // H
FF = 512
ED = 64
NB = 26
NP = NB * P
PAIRS = NB // 2
J = 16
G = 26
T = J * G
EP = T * P
CH = G * P
HALF = G // 2
UNIT = HALF * P
BW = 10 * D
BIG = 3e38
START = 32
EPS = 1e-5


def build(nc, a, out):
    kv_table = nc.dram_tensor("kv_table", (NP, 2 * D), F32, kind="Internal").ap()
    v_edges = nc.dram_tensor("v_edges", (P, T * D), F32, kind="Internal").ap()
    rel_dram = nc.dram_tensor("rel_dram", (G, J * P), BF16, kind="Internal").ap()
    block_dram = nc.dram_tensor("block_dram", (G, J), I32, kind="Internal").ap()

    with ExitStack() as ctx:
        def sb(name, shape, dt=F32):
            return ctx.enter_context(nc.sbuf_tensor(name, shape, dt))

        def sem(name):
            return ctx.enter_context(nc.semaphore(name))

        X = sb("X", [P, NP])
        Y = sb("Y", [P, NP])
        QT = sb("QT", [P, NP + P])
        AG1 = sb("AG1", [P, NP + P])
        KV = sb("KV", [P, 2, J, 2 * D])
        OHT = sb("OHT", [P, 2, 2, 8 * P])
        REL = sb("REL", [P, 2, J * P], BF16)
        LB = sb("LB", [P, CH])
        FB = sb("FB", [P, CH])
        MB = sb("MB", [P, CH])
        AE = MB
        ADD_P = sb("ADD_P", [P, CH], BF16)
        ADD_N = sb("ADD_N", [P, CH], BF16)
        SAME_P = sb("SAME_P", [P, CH], U8)
        SAME_N = sb("SAME_N", [P, CH], U8)
        LOOP1 = sb("LOOP1", [P, CH], U8)
        idx = sb("idx", [P, 2, J], U32)
        dst_first = sb("dst_first", [P, T], I32)
        rel_edge = sb("rel_edge", [P, T])
        block_row = sb("block_row", [1, T], I32)
        first_row = sb("first_row", [1, 2 * J * 16], I32)
        iota_row = sb("iota_row", [P, P])
        iota_part = sb("iota_part", [P, 2])
        ident = sb("ident", [P, P])
        ones = sb("ones", [1, P])
        ones3 = sb("ones3", [3, P], BF16)
        Wp = [sb("Wp0", [P, 3 * D]), sb("Wp1", [P, 4 * D])]
        BIAS = sb("BIAS", [3, BW], BF16)
        Bp = [BIAS[:, 0:3 * D], BIAS[:, 3 * D:7 * D]]
        bo = BIAS[:, 7 * D:8 * D]
        bf2 = [BIAS[:, (8 + l) * D:(9 + l) * D] for l in range(2)]
        Wo = sb("Wo", [P, D])
        We = sb("We", [ED, D])
        W1 = [sb(f"W1{l}", [P, FF]) for l in range(2)]
        W2 = [sb(f"W2{l}", [P, 4, D]) for l in range(2)]
        bf1 = [sb(f"bf1{l}", [P, 4]) for l in range(2)]
        gb = sb("gb", [P, 4])
        GB = sb("GB", [P, 4, D])
        MEAN = sb("MEAN", [P, NB])
        RS = sb("RS", [P, NB])
        SD = sb("SD", [P, NB])
        BN = sb("BN", [P, NB, 6])
        cols = sb("cols", [P, 4])
        grow = sb("grow", [1, 4, P])
        srow = sb("srow", [1, 2, P + 2])
        TMP = sb("TMP", [P, 1280])

        PS = [ctx.enter_context(nc.psum_tensor(f"PS{b}", [P, 512], F32)) for b in range(8)]

        xn = [TMP[:, k * D:(k + 1) * D] for k in range(2)]
        hN = [TMP[:, 256 + k * D:256 + (k + 1) * D] for k in range(2)]
        hT = [TMP[:, 512 + k * P:512 + (k + 1) * P] for k in range(2)]
        kv_out = [KV[:, 0, k, :] for k in range(2)]
        gT = [KV[:, 1, 2 * k:2 * k + 2, :].rearrange("p a (b n) -> p (a b) n", b=2) for k in range(2)]
        bias_raw = TMP[0:3, 0:BW]
        bias_hi = MB[0:3, 0:BW // 2].bitcast(BF16)
        bias_mid = MB[0:3, BW // 2:BW].bitcast(BF16)
        bias_lo = MB[0:3, BW:3 * BW // 2].bitcast(BF16)
        bias_rest = MB[0:3, 3 * BW // 2:5 * BW // 2]
        AG2 = OHT[:, :, :, :].rearrange("p a b n -> p (a b n)")[:, 0:NP + P]
        AGG = [QT, AG1, AG2]
        prod = [FB[:, r * 512:(r + 1) * 512] for r in range(4)]
        Ls = [TMP[:, 1024 + s * P:1024 + (s + 1) * P] for s in range(2)]
        ea = [AG1[0:ED, hh * 8 * P:(hh + 1) * 8 * P] for hh in range(2)]
        kv_flat = KV[:, :, :, :].rearrange("p s j d -> p (s j d)")
        dstB = AG1[:, 0:CH + 2].bitcast(I32)
        srcB = Y[:, 0:CH].bitcast(I32)
        is_loop = MB
        loops = Y[:, 0:CH]
        V4 = [kv_flat[:, u * UNIT:(u + 1) * UNIT] for u in range(4)]
        OH4 = [LB[:, 0:UNIT], LB[:, UNIT:2 * UNIT], FB[:, 0:UNIT], FB[:, UNIT:2 * UNIT]]
        ae4 = AE[:, :].rearrange("p (g h j) -> p g h j", g=G, h=H)
        dstG = OHT[0:G, 0, :, :].rearrange("p a n -> p (a n)").bitcast(I32)
        relG = REL[0:G, 0, :]
        blkG = OHT[0:G, 1, 0, 0:J].bitcast(I32)
        dst_edge = OHT[:, 1, 1, 0:T].bitcast(I32)

        S = {n: sem(n) for n in """x_loaded dstg_loaded dste_loaded chunks_loaded first_weights weights_loaded
            rel_stored block_loaded out_stored""".split()}
        counts = """consts_made rel_made prep_step kv_copied kv_free v_free gates_made
            pool_go rel_begun stat_step moment_step var_ready sd_ready rs_ready
            xn_ready tp_ready ht_ready proj_ready q_made x_kept
            ln_affine ln_last half_sum sum_ready att_ready res_ready hidden_ready gelu_ready ffn_ready ffn_added
            out_made bias_made bias_step x_summed x_out
            oht_ready qe_ready prod_done e_ready e_used l_ready lt_ready lb_ready logits_done batch_step
            xc_col xc_row xc_scanned xc_back soft_step shifted exp_ready aet_ready aet_used
            agg_zeroed sum0_ready sum1_ready sum1_added act_col
            """.split()
        S.update((n, sem(n)) for n in counts)

        def values(row, at, n, engine, most):
            return nc.values_load_multi_w_load_instructions(row[0:1, ds(at, n)], engines=(engine,), min_val=0, max_val=most,
                                                               skip_runtime_bounds_check_because="they come from dst, which holds indices of nodes")[1]

        def pipelined(eng, *stages):
            top = max(ahead for f, ahead in stages)

            def step(n, first, k):
                for f, ahead in stages:
                    if first is None or 0 <= first + ahead < NB:
                        f(n + ahead, (k + ahead) % 2)

            for n in range(-top, 0):
                step(n, n, n)
            trips = (NB - top) // 2
            with eng.Fori(0, trips) as i:
                for k in range(2):
                    step(i * 2 + k, None, k)
            for n in range(2 * trips, NB):
                step(n, n, n)

        def done(name, n):
            return S[name], n + START

        kv_stored = [sem(f"kv_stored{k}") for k in range(2)]
        idx_loaded = [sem(f"idx_loaded{s}") for s in range(2)]
        rel_loaded = [sem(f"rel_loaded{s}") for s in range(2)]
        ea_loaded = [sem(f"ea_loaded{s}") for s in range(2)]
        gathered = [[sem(f"gathered{s}{hh}") for hh in range(2)] for s in range(2)]
        v_stored = [[sem(f"v_stored{s}{hh}") for hh in range(2)] for s in range(2)]
        v_loaded = [sem(f"v_loaded{u}") for u in range(4)]
        pv_ready = [sem(f"pv_ready{u}") for u in range(4)]
        oh_ready = [sem(f"oh_ready{u}") for u in range(4)]

        class Steps:

            def __init__(self, eng, name):
                self.eng, self.s, self.base, self.n = eng, S[name], 0, 0
                self.i, self.per = 0, 0

            def loop(self, i, per):
                self.base, self.n, self.i, self.per = self.base + self.n, 0, i, per

            def end(self, trips):
                assert self.n == self.per, (self.n, self.per)
                self.base, self.n, self.i, self.per = self.base + trips * self.per, 0, 0, 0

            def run(self, ins):
                ins.then_inc(self.s, 1)
                self.n += 1
                self.eng.wait_ge(self.s, self.i * self.per + (self.base + self.n + START))

        block = ctx.enter_context(nc.Block())

        @block.sync
        def _(sp):
            sp.dma_start(X[:, :].rearrange("p (b d) -> p b d", b=NB), a["x"].rearrange("(b p) d -> p b d", p=P)).then_inc(S["x_loaded"], 16)
            sp.dma_start(dstG.rearrange("g (j e) -> g j e", j=J),
                         a["dst"][1:EP + 1].rearrange("(j g e) -> g j e", j=J, g=G)).then_inc(S["dstg_loaded"], 16)
            sp.dma_start(dst_edge, a["dst_edge"]).then_inc(S["dste_loaded"], 16)
            sp.dma_start(dst_first[:, :], a["dst_first"].rearrange("(a t) -> a t", a=1).broadcast_to([P, T])).then_inc(S["dste_loaded"], 16)
            row = lambda v: v.rearrange("(a n) -> a n", a=1)
            biases = ["L0_gnn_bq", "L0_gnn_bk", "L0_gnn_bv", "L1_gnn_bq", "L1_gnn_bk", "L1_gnn_bv", "L1_gnn_bskip", "L0_gnn_bo",
                      "L0_gnn_bf2", "L1_gnn_bf2"]
            for n, name in enumerate(biases):
                sp.dma_start(bias_raw[:, n * D:(n + 1) * D], row(a[name]).broadcast_to([3, D])).then_inc(S["first_weights"], 16)

            sp.wait_ge(*done("rel_made", 2))
            sp.dma_start(rel_dram, relG).then_inc(S["rel_stored"], 16)
            sp.dma_start(block_dram, blkG).then_inc(S["rel_stored"], 16)
            sp.wait_ge(S["rel_stored"], 32)
            sp.dma_start(first_row[:, :], a["dst_units"].rearrange("(a n) -> a n", a=1)).then_inc(S["block_loaded"], 16)
            for h in range(H):
                sp.dma_start(dstB[h * J:(h + 1) * J, :],
                             bass.AP(a["dst"].tensor, 0, [[CH, J], [1, CH + 2]])).then_inc(S["chunks_loaded"], 16)
                sp.dma_start(srcB[h * J:(h + 1) * J, :],
                             a["src"].rearrange("(j n) -> j n", j=J)).then_inc(S["chunks_loaded"], 16)
            sp.dma_start(block_row[:, :], block_dram.rearrange("g j -> (g j)").rearrange("(a n) -> a n", a=1)).then_inc(S["block_loaded"], 16)

            for l in range(2):
                with sp.Fori(0, PAIRS) as i:
                    for k in range(2):
                        sp.wait_ge(*done("kv_copied", i * 2 + (l * NB + k + 1)))
                        sp.dma_start(kv_table[ds(i * 256 + k * P, P), :], kv_out[k]).then_inc(kv_stored[k], 16)
                    for k in range(2):
                        sp.wait_ge(kv_stored[k], i * 16 + 16 * (PAIRS * l + 1))
                        sp.sem_inc(S["kv_free"], 1)
                with sp.Fori(0, PAIRS) as i:
                    for s in range(2):
                        sp.wait_ge(*done("l_ready", i * 8 + (8 * PAIRS * l + 4 * s - 4)))
                        sp.dma_start(idx[:, s, :], a["src_batch"][ds(i * 2 + s, 1), :, :].rearrange("a p j -> (a p) j")).then_inc(idx_loaded[s], 16)
                        sp.wait_ge(*done("oht_ready", i * 8 + (8 * PAIRS * l + 4 * s - 4)))
                        sp.sem_inc(S["rel_begun"], 1)
                        sp.dma_start(REL[:, s, :], rel_dram[ds(i * 2 + s, 1), :].broadcast_to([P, J * P])).then_inc(rel_loaded[s], 16)
                        if l:
                            for hh in range(2):
                                sp.wait_ge(*done("e_ready", i * 8 + (4 * s + 2 * hh - 2)))
                                sp.dma_start(ea[hh], a["edge_batch"][ds(i * 2 + s, 1), :, hh * 8 * P:(hh + 1) * 8 * P]
                                             .rearrange("a p j -> (a p) j")).then_inc(ea_loaded[hh], 16)
                for s in range(2):
                    for hh in range(2):
                        sp.wait_ge(v_stored[s][hh], 16 * PAIRS * (l + 1))
                    sp.wait_ge(*done("logits_done", l + 1))
                with sp.Fori(0, J // 2) as i:
                    for q in range(2):
                        for st in range(2):
                            u = 2 * st + q
                            sp.wait_ge(*done(f"sum{st}_ready", i * 8 + (64 * l + 4 * q - 4)))
                            sp.dma_start(V4[u], v_edges[:, ds(i * (G * P) + (st * (J // 2) * G + q * HALF) * P, UNIT)]).then_inc(v_loaded[u], 16)
            full = N // P
            for b0, b1 in ((0, NB // 2), (NB // 2, full)):
                sp.wait_ge(*done("out_made", NB if b1 == full else b1))
                sp.dma_start(out[b0 * P:b1 * P, :].rearrange("(b p) d -> p b d", p=P),
                             Y[:, b0 * P:b1 * P].rearrange("p (b d) -> p b d", b=b1 - b0)).then_inc(S["out_stored"], 16)
            sp.dma_start(out[full * P:N, :], Y[0:N - full * P, full * P:(full + 1) * P]).then_inc(S["out_stored"], 16)
            sp.wait_ge(S["out_stored"], 48)

        @block.gpsimd
        def _(pool):
            g = nc.gpsimd
            g.memset(ones[:, :], 1.0).then_inc(S["consts_made"], 1)
            g.memset(ones3[:, :], 1.0).then_inc(S["consts_made"], 1)
            g.memset(ident[:, :], 0.0).then_inc(S["consts_made"], 1)
            g.memset(srow[:, :, :], 0.0).then_inc(S["consts_made"], 1)
            g.memset(QT[:, NP:NP + P], 0.0).then_inc(S["consts_made"], 1)
            pool.wait_ge(*done("consts_made", 5))
            g.affine_select(out=ident[:, :], in_=ident[:, :], compare_op=ALU.not_equal, fill=1.0,
                            base=0, pattern=[[-1, P]], channel_multiplier=1).then_inc(S["consts_made"], 1)
            g.iota(iota_row[:, :], pattern=[[1, P]], base=0, channel_multiplier=0,
                   allow_small_or_imprecise_dtypes=True).then_inc(S["consts_made"], 1)
            g.iota(iota_part[:, :], pattern=[[P, 2]], base=0, channel_multiplier=1,
                   allow_small_or_imprecise_dtypes=True).then_inc(S["consts_made"], 1)

            pool.wait_ge(S["weights_loaded"], 16 * WEIGHTS)
            for l in range(2):
                if l:
                    with pool.Fori(0, PAIRS) as i:
                        for k in range(2):
                            pool.wait_ge(*done("xn_ready", i * 2 + (2 * NB + k + 1)))
                            pool.sem_inc(S["pool_go"], 1)
                            g.tensor_copy(X[:, ds(i * 256 + k * P, P)], xn[k]).then_inc(S["x_kept"], 1)
                for k in range(2):
                    pool.wait_ge(kv_stored[k], 16 * PAIRS * (l + 1))
                with pool.Fori(0, PAIRS) as i:
                    for s in range(2):
                        pool.wait_ge(idx_loaded[s], i * 16 + 16 * (PAIRS * l + 1))
                        for hh in range(2):
                            pool.wait_ge(*done("l_ready", i * 8 + (8 * PAIRS * l + 4 * s + 2 * hh - 6)))
                            pool.wait_ge(*done("v_free", i * 4 + (2 * NB * l + 2 * s + hh - 3)))
                            pool.sem_inc(S["pool_go"], 1)
                            for j in range(hh * 8, hh * 8 + 8):
                                g.indirect_dma_start(KV[:, s, j, :], None, kv_table,
                                                     bass.IndirectOffsetOnAxis(ap=idx[:, s, j:j + 1], axis=0)).then_inc(gathered[s][hh], 16)
                pool.wait_ge(*done("logits_done", l + 1))
                for sums in AGG:
                    g.memset(sums[:, :], 0.0).then_inc(S["agg_zeroed"], 1)
                pool.wait_ge(*done("aet_used", 7 * (l + 1)))
                with pool.Fori(0, J // 2) as i:
                    for q in range(2):
                        for st in range(2):
                            u = 2 * st + q
                            pool.wait_ge(v_loaded[u], i * 16 + 16 * (l * 8 + 1))
                            pool.sem_inc(S["pool_go"], 1)
                            v4 = V4[u].rearrange("p (m h c) -> p m h c", m=HALF, h=H)
                            at = ae4[:, q * HALF:(q + 1) * HALF, :, ds(i + 8 * st, 1)].broadcast_to([P, HALF, H, C])
                            g.tensor_tensor(v4, v4, at, ALU.mult).then_inc(pv_ready[u], 1)
                if l == 0:
                    with pool.Fori(0, NB) as n:
                        pool.wait_ge(*done("res_ready", n + 1))
                        at = ds(n * P, P)
                        pool.sem_inc(S["pool_go"], 1)
                        g.tensor_tensor(X[:, at], X[:, at], Y[:, at], ALU.add).then_inc(S["x_summed"], 1)
                else:
                    with pool.Fori(0, PAIRS) as i:
                        for k in range(2):
                            at = ds(i * 256 + k * P, P)
                            pool.wait_ge(*done("xn_ready", i * 2 + (3 * NB + k + 1)))
                            pool.sem_inc(S["pool_go"], 1)
                            g.tensor_tensor(Y[:, at], xn[k], GB[:, 0, :], ALU.mult).then_inc(S["ln_affine"], 1)
                            pool.wait_ge(*done("ln_affine", i * 6 + (3 * k + 1)))
                            pool.sem_inc(S["pool_go"], 1)
                            g.tensor_tensor(Y[:, at], Y[:, at], GB[:, 1, :], ALU.add).then_inc(S["ln_affine"], 1)
                            pool.wait_ge(*done("ln_affine", i * 6 + (3 * k + 2)))
                            pool.wait_ge(*done("tp_ready", i * 2 + (3 * NB + k - 1)))
                            pool.sem_inc(S["pool_go"], 1)
                            g.tensor_copy(hN[k], Y[:, at]).then_inc(S["ln_affine"], 1)
                    with pool.Fori(0, PAIRS) as i:
                        for k in range(2):
                            pool.wait_ge(*done("xn_ready", i * 2 + (4 * NB + k + 1)))
                            pool.wait_ge(*done("x_out", i * 2 + (k - 1)))
                            g.tensor_tensor(hN[k], xn[k], GB[:, 2, :], ALU.mult).then_inc(S["ln_last"], 1)
                            pool.wait_ge(*done("ln_last", i * 4 + (2 * k + 1)))
                            g.tensor_tensor(hN[k], hN[k], GB[:, 3, :], ALU.add).then_inc(S["ln_last"], 1)

        @block.scalar
        def _(act):
            sc = nc.scalar

            def roots(n):
                act.wait_ge(*done("var_ready", n))
                sc.activation(SD[:, :], RS[:, :], ACT.Sqrt).then_inc(S["sd_ready"], 1)

            def w(dst, src, name="weights_loaded"):
                act.dma_start(dst, src).then_inc(S[name], 16)

            row = lambda v: v.rearrange("(a n) -> a n", a=1)
            col = lambda v: v.rearrange("(n a) -> n a", a=1)
            for n, q in enumerate(("q", "k", "v")):
                w(Wp[0][:, n * D:(n + 1) * D], a[f"L0_gnn_W{q}"], "first_weights")
            for n, v in enumerate(("g1", "b1", "g2", "b2")):
                w(gb[:, n:n + 1], col(a[f"L0_gnn_{v}"]), "first_weights")
            for n, q in enumerate(("q", "k", "v", "skip")):
                w(Wp[1][:, n * D:(n + 1) * D], a[f"L1_gnn_W{q}"])
            w(Wo[:, :], a["L0_gnn_Wo"])
            w(We[:, :], a["L1_gnn_We"])
            for l, f in ((0, ""), (1, "f")):
                w(W1[l][:, :], a[f"L{l}_gnn_W{f}1"])
                w(W2[l][:, :, :], a[f"L{l}_gnn_W{f}2"].rearrange("(c k) n -> k c n", k=P))
                for c in range(4):
                    w(bf1[l][:, c:c + 1], col(a[f"L{l}_gnn_bf1"][c * P:(c + 1) * P]))
            for n, v in enumerate(("g1", "b1", "g2", "b2")):
                w(GB[:, n, :], row(a[f"L1_gnn_{v}"]).broadcast_to([P, D]))

            act.wait_ge(S["first_weights"], 16 * FIRST_WEIGHTS)
            for l in range(2):
                if l == 0:
                    roots(1)
                def turned(n, k):
                    act.wait_ge(*done("tp_ready", n + (2 * NB * l + 1)))
                    act.wait_ge(*done("proj_ready", n + (NB * l - 1)))
                    if l == 0:
                        sc.activation(hT[k], PS[k][:, 0:P], ACT.Identity, bias=gb[:, 1:2], scale=gb[:, 0:1]).then_inc(S["ht_ready"], 1)
                    else:
                        sc.activation(hT[k], PS[k][:, 0:P], ACT.Copy).then_inc(S["ht_ready"], 1)

                def keys_values(n, k):
                    act.wait_ge(*done("q_made", n + (NB * l + 1)))
                    act.wait_ge(*done("kv_free", n + (NB * l - 1)))
                    sc.activation(kv_out[k], PS[2 + k][:, D:3 * D], ACT.Copy).then_inc(S["kv_copied"], 1)

                pipelined(act, (turned, 2), (keys_values, 0))
                with act.Fori(0, PAIRS) as i:
                    for s in range(2):
                        def free(hh):
                            act.wait_ge(v_stored[s][hh], i * 16 + 16 * (PAIRS * l + 1))
                            act.sem_inc(S["v_free"], 1)

                        for hh in range(2):
                            if l == 0:
                                act.wait_ge(gathered[s][hh], i * 128 + 128)
                            else:
                                act.wait_ge(*done("e_used", i * 8 + (4 * s + 2 * hh + 2)))
                            act.dma_start(v_edges.rearrange("p (j n) -> p j n", j=J)[:, hh * 8:hh * 8 + 8, ds(i * 256 + s * P, P)],
                                          KV[:, s, hh * 8:hh * 8 + 8, D:2 * D]).then_inc(v_stored[s][hh], 16)
                        free(0)
                        act.wait_ge(*done("lt_ready", i * 2 + (NB * l + s + 1)))
                        sc.activation(LB[:, ds(i * 256 + s * P, P)], PS[6][:, s * P:(s + 1) * P], ACT.Copy).then_inc(S["lb_ready"], 1)
                        free(1)
                act.wait_ge(*done("shifted", l + 1))
                sc.activation(LB[:, :], LB[:, :], ACT.Exp).then_inc(S["exp_ready"], 1)
                for b in range(0, G, 4):
                    act.wait_ge(*done("aet_ready", 7 * l + b // 4 + 1))
                    w_ = min(4, G - b) * P
                    sc.activation(AE[:, b * P:b * P + w_], PS[b // 4 % 4][:, 0:w_], ACT.Copy).then_inc(S["aet_used"], 1)
                act.wait_ge(*done("agg_zeroed", 3 * (l + 1)))
                with act.Fori(0, J // 2) as i:
                    for q in range(2):
                        for m in range(HALF):
                            n = q * HALF + m
                            if m % 4 == 0:
                                firsts = values(first_row, i * 32 + (q * 16 + m), min(4, HALF - m), ENG.Activation, N)
                                act.wait_ge(*done("sum0_ready", i * 8 + (l * 64 + q * 4 + m // 4 + 1)))
                            first = firsts[m % 4]
                            p = PS[m // 4][:, m % 4 * P:(m % 4 + 1) * P]
                            act.wait_ge(*done("act_col", i * (2 * G) + (l * 16 * G + 2 * n)))
                            sc.activation(QT[:, ds(first, 1)], p[:, 0:1], ACT.Identity, bias=QT[:, ds(first, 1)]).then_inc(S["act_col"], 1)
                            sc.activation(QT[:, ds(first + 1, P - 1)], p[:, 1:P], ACT.Copy).then_inc(S["act_col"], 1)
                roots(2 if l == 0 else 4)
                def gelus(n, k):
                    act.wait_ge(*done("hidden_ready", n + (NB * l + 1)))
                    act.wait_ge(*done("ffn_ready", n + (NB * l - 1)))
                    for c in range(4):
                        sc.activation(gT[k][:, c, :], PS[2 + k][:, c * P:(c + 1) * P], ACT.Gelu,
                                      bias=bf1[l][:, c:c + 1]).then_inc(S["gelu_ready"], 1)

                act.wait_ge(S["weights_loaded"], 16 * WEIGHTS)
                gelus(0, 0)
                gelus(1, 1)
                with act.Fori(1, PAIRS) as i:
                    for k in range(2):
                        gelus(i * 2 + k, k)
                roots(3 if l == 0 else 5)
            roots(6)

        @block.tensor
        def _(pe):
            te = nc.tensor
            for n in counts:
                pe.sem_inc(S[n], START)
            xc = [0]

            def exchange(col, part):
                xc[0] += 1
                pe.wait_ge(*done("xc_col", xc[0]))
                te.matmul(PS[7][0:1, 0:P], col, ident[:, :], start=True, stop=True).then_inc(S["xc_row"], 1)
                pe.wait_ge(*done("xc_scanned", xc[0]))
                te.matmul(PS[7][:, P:P + 1], part, ones[0:1, 0:1], start=True, stop=True).then_inc(S["xc_back"], 1)

            fwd, bwd = srow[0:1, 0, 0:P], srow[0:1, 1, 1:P + 1]

            pe.wait_ge(*done("consts_made", 8))
            pe.wait_ge(S["first_weights"], 16 * FIRST_WEIGHTS)
            pe.wait_ge(*done("bias_made", 1))

            for l in range(2):
                Wd = (3 + l) * D

                def turn(n, k):
                    pe.wait_ge(*done("xn_ready", n + (2 * NB * l + 1)))
                    pe.wait_ge(*done("ht_ready", n + (2 * NB * l - 1)))
                    te.transpose(PS[k][:, 0:P], xn[k], ident[:, :]).then_inc(S["tp_ready"], 1)

                def project(n, k):
                    pe.wait_ge(*done("ht_ready", n + (2 * NB * l + 1)))
                    pe.wait_ge(*done("kv_copied", n + (NB * l - 1)))
                    te.matmul(PS[2 + k][:, 0:Wd], ones3[:, :], Bp[l], start=True, stop=False)
                    te.matmul(PS[2 + k][:, 0:Wd], hT[k], Wp[l][:, :], start=False, stop=True).then_inc(S["proj_ready"], 1)

                pipelined(pe, (turn, 2), (project, 0))
                pe.wait_ge(S["block_loaded"], 32)
                pe.wait_ge(*done("q_made", NB * (l + 1)))
                pe.wait_ge(*done("kv_copied", NB * (l + 1)))
                pe.wait_ge(S["weights_loaded"], 16 * WEIGHTS)
                def logits(i):
                    for s in range(2):
                        for q4 in range(4):
                            hh = q4 // 2
                            if q4 % 2 == 0:
                                pe.wait_ge(*done("oht_ready", i * 8 + (8 * PAIRS * l + 4 * s + 2 * hh + 2)))
                                if l:
                                    pe.wait_ge(ea_loaded[hh], i * 32 + 16 * (s + 1))
                            blks = values(block_row, i * 2 * J + (s * J + 4 * q4), 4, ENG.PE, NP - P)
                            pe.wait_ge(*done("prod_done", i * 8 + (8 * PAIRS * l + 4 * s + q4 - 3)))
                            for jj in range(4):
                                j = 4 * q4 + jj
                                blk = blks[jj]
                                o = PS[q4][:, jj * P:(jj + 1) * P]
                                e0 = (j % 8) * P
                                te.matmul(o, OHT[:, hh, 0, e0:e0 + P], QT[:, ds(blk, P)], start=True, stop=False)
                                last = te.matmul(o, OHT[:, hh, 1, e0:e0 + P], QT[:, ds(blk + P, P)], start=False, stop=True)
                            last.then_inc(S["qe_ready"], 1)
                            if l:
                                pe.wait_ge(*done("e_used", i * 8 + (4 * s + q4 - 1)))
                                for jj in range(4):
                                    e0 = ((4 * q4 + jj) % 8) * P
                                    last = te.matmul(PS[4 + q4 % 2][:, jj * P:(jj + 1) * P], ea[hh][:, e0:e0 + P], We[:, :], start=True, stop=True)
                                last.then_inc(S["e_ready"], 1)
                        pe.wait_ge(*done("l_ready", i * 8 + (8 * PAIRS * l + 4 * s + 4)))
                        pe.wait_ge(*done("lb_ready", i * 2 + (NB * l + s)))
                        te.transpose(PS[6][:, s * P:(s + 1) * P], Ls[s], ident[:, :]).then_inc(S["lt_ready"], 1)

                if l == 0:
                    with pe.Fori(0, 10) as i:
                        logits(i)
                    pe.wait_ge(*done("prep_step", 3))
                    te.matmul(PS[7][0:1, 0:P], cols[:, 0:1], ident[:, :], start=True, stop=True)
                    te.matmul(PS[7][0:1, P:2 * P], cols[:, 1:2], ident[:, :], start=True, stop=True).then_inc(S["xc_row"], 1)
                    exchange(loops[:, CH - 1:CH], fwd)
                with pe.Fori(10 if l == 0 else 0, PAIRS) as i:
                    logits(i)
                exchange(FB[:, CH - 1:CH], fwd)
                exchange(MB[:, 0:1], bwd)
                exchange(FB[:, CH - 1:CH], fwd)
                exchange(MB[:, 0:1], bwd)
                pe.wait_ge(*done("soft_step", SOFT * (l + 1)))
                for b in range(0, G, 4):
                    if b >= 16:
                        pe.wait_ge(*done("aet_used", 7 * l + b // 4 - 3))
                    for n in range(b, min(b + 4, G)):
                        last = te.transpose(PS[b // 4 % 4][:, (n - b) * P:(n - b + 1) * P], LB[:, n * P:(n + 1) * P], ident[:, :])
                    last.then_inc(S["aet_ready"], 1)
                pe.wait_ge(*done("aet_used", 7 * (l + 1)))
                with pe.Fori(0, J // 2) as i:
                    for q in range(2):
                        for st in range(2):
                            pe.wait_ge(oh_ready[2 * st + q], i + (l * (J // 2) + 1))
                            pe.wait_ge(pv_ready[2 * st + q], i + (l * (J // 2) + 1))
                        for b in range(4):
                            for st in range(2):
                                u = 2 * st + q
                                tiles = (l * 8 * G + (q - 1) * HALF) + min(4 * b + 4, HALF)
                                if st == 0:
                                    pe.wait_ge(*done("act_col", i * (2 * G) + 2 * tiles))
                                else:
                                    pe.wait_ge(*done("sum1_added", i * G + tiles))
                                for m in range(4 * b, min(4 * b + 4, HALF)):
                                    last = te.matmul(PS[4 * st + b][:, m % 4 * P:(m % 4 + 1) * P],
                                                     V4[u][:, m * P:(m + 1) * P], OH4[u][:, m * P:(m + 1) * P], start=True, stop=True)
                                last.then_inc(S[f"sum{st}_ready"], 1)
                pe.wait_ge(*done("act_col", 16 * G * (l + 1)))
                pe.wait_ge(*done("sum1_added", 8 * G * (l + 1)))
                def attend(n, k):
                    pe.wait_ge(*done("sum_ready", n + (NB * l + 1)))
                    pe.wait_ge(*done("res_ready", n + (NB * l - 1)))
                    if l == 0:
                        te.matmul(PS[k][:, 0:P], ones3[:, :], bo, start=True, stop=False)
                        te.matmul(PS[k][:, 0:P], xn[k], Wo[:, :], start=False, stop=True).then_inc(S["att_ready"], 1)
                    else:
                        te.transpose(PS[k][:, 0:P], xn[k], ident[:, :]).then_inc(S["att_ready"], 1)

                with pe.Fori(0, PAIRS) as i:
                    for k in range(2):
                        attend(i * 2 + k, k)
                pe.wait_ge(*done("res_ready", NB * (l + 1)))

                def turn2(n, k):
                    if l == 0:
                        pe.wait_ge(*done("xn_ready", n + (NB + 1)))
                    else:
                        pe.wait_ge(*done("ln_affine", n * 3 + 3))
                    pe.wait_ge(*done("ht_ready", n + ((2 * l + 1) * NB - 1)))
                    te.transpose(PS[k][:, 0:P], (hN if l else xn)[k], ident[:, :]).then_inc(S["tp_ready"], 1)

                def widen(n, k):
                    pe.wait_ge(*done("ht_ready", n + ((2 * l + 1) * NB + 1)))
                    pe.wait_ge(*done("gelu_ready", n * 4 + (4 * NB * l - 4)))
                    for c in range(4):
                        last = te.matmul(PS[2 + k][:, c * P:(c + 1) * P], W1[l][:, c * P:(c + 1) * P], hT[k], start=True, stop=True)
                    last.then_inc(S["hidden_ready"], 1)

                def narrow(n, k):
                    pe.wait_ge(*done("gelu_ready", n * 4 + (4 * NB * l + 4)))
                    pe.wait_ge(*done("ffn_added", n + (NB * l - 1)))
                    o = PS[4 + k][:, 0:P]
                    te.matmul(o, ones3[:, :], bf2[l], start=True, stop=False)
                    for c in range(4):
                        last = te.matmul(o, gT[k][:, c, :], W2[l][:, c, :], start=False, stop=(c == 3))
                    last.then_inc(S["ffn_ready"], 1)

                pipelined(pe, (turn2, 2), (widen, 1), (narrow, 0))
                pe.wait_ge(*done("ffn_added", NB * (l + 1)))

        @block.vector
        def _(dve):
            v = nc.vector
            xc = [0]

            def scan(o, gate, data, init, op0, op1):
                return v.tensor_tensor_scan(o, gate, data, init, op0, op1)

            def exchange(forward, gate, op0, op1):
                xc[0] += 1
                dve.wait_ge(*done("xc_row", xc[0] + 1))
                if forward:
                    scan(srow[0:1, 0, 1:P + 1], grow[0:1, gate, :], PS[7][0:1, 0:P], 0.0, op0, op1).then_inc(S["xc_scanned"], 1)
                else:
                    scan(srow[0:1, 1, 0:P][:, ::-1], grow[0:1, gate, ::-1], PS[7][0:1, 0:P][:, ::-1], 0.0, op0, op1).then_inc(S["xc_scanned"], 1)
                dve.wait_ge(*done("xc_back", xc[0]))
                return v.tensor_copy(cols[:, 2:3], PS[7][:, P:P + 1])

            def block_stats(src, n):
                dve.wait_ge(S["x_loaded"], 16)
                v.bn_stats(BN[:, ds(n, 1), :].rearrange("p a c -> p (a c)"), src[:, ds(n * P, P)]).then_inc(S["stat_step"], 1)

            def inv_std(n):
                dve.wait_ge(*done("stat_step", NB * n))
                even, odd = BN[:, :, 1], BN[:, :, 4]
                v.tensor_tensor(MEAN[:, :], even, odd, ALU.add).then_inc(S["moment_step"], 1)
                v.tensor_tensor(SD[:, :], even, odd, ALU.subtract).then_inc(S["moment_step"], 1)
                v.tensor_tensor(RS[:, :], BN[:, :, 2], BN[:, :, 5], ALU.add).then_inc(S["moment_step"], 1)
                dve.wait_ge(*done("moment_step", 7 * n - 4))
                v.tensor_scalar(MEAN[:, :], MEAN[:, :], 0.5, None, ALU.mult).then_inc(S["moment_step"], 1)
                v.scalar_tensor_tensor(SD[:, :], SD[:, :], 0.25, SD[:, :], ALU.mult, ALU.mult).then_inc(S["moment_step"], 1)
                v.tensor_scalar(RS[:, :], RS[:, :], 1.0 / D, EPS, ALU.mult, ALU.add).then_inc(S["moment_step"], 1)
                dve.wait_ge(*done("moment_step", 7 * n - 1))
                v.tensor_tensor(RS[:, :], RS[:, :], SD[:, :], ALU.add).then_inc(S["moment_step"], 1)
                dve.wait_ge(*done("moment_step", 7 * n))
                dve.sem_inc(S["var_ready"], 1)
                dve.wait_ge(*done("sd_ready", n))
                v.reciprocal(RS[:, :], SD[:, :]).then_inc(S["rs_ready"], 1)
                dve.wait_ge(*done("rs_ready", n))

            def normalise(o, src, n):
                return v.tensor_scalar(o, src[:, ds(n * P, P)], MEAN[:, ds(n, 1)], RS[:, ds(n, 1)], ALU.subtract, ALU.mult)

            dve.wait_ge(S["dstg_loaded"], 16)
            g3 = dstG.rearrange("g (j e) -> g j e", j=J)
            v.tensor_scalar(blkG, g3[:, :, 0], 7, 7, ALU.logical_shift_right, ALU.logical_shift_left).then_inc(S["rel_made"], 1)
            dve.wait_ge(*done("rel_made", 1))
            v.tensor_tensor(relG.rearrange("g (j e) -> g j e", j=J), g3, blkG.unsqueeze(2).broadcast_to([G, J, P]), ALU.subtract)\
                .then_inc(S["rel_made"], 1)
            dve.wait_ge(S["dste_loaded"], 32)
            v.tensor_tensor(rel_edge[:, :], dst_edge, dst_first[:, :], ALU.subtract).then_inc(S["rel_made"], 1)
            dve.wait_ge(S["first_weights"], 16 * FIRST_WEIGHTS)
            dve.wait_ge(*done("consts_made", 8))
            prep = Steps(dve, "bias_step")
            prep.run(v.tensor_copy(bias_hi, bias_raw))
            prep.run(v.tensor_tensor(bias_rest, bias_raw, bias_hi, ALU.subtract))
            prep.run(v.tensor_copy(bias_mid, bias_rest))
            prep.run(v.tensor_tensor(bias_lo, bias_rest, bias_mid, ALU.subtract))
            prep.run(v.tensor_scalar(BIAS[:, :], bias_hi, ident[0:3, 0:1], None, ALU.mult))
            prep.run(v.scalar_tensor_tensor(BIAS[:, :], bias_mid, ident[0:3, 1:2], BIAS[:, :], ALU.mult, ALU.add))
            prep.run(v.scalar_tensor_tensor(BIAS[:, :], bias_lo, ident[0:3, 2:3], BIAS[:, :], ALU.mult, ALU.add))
            dve.sem_inc(S["bias_made"], 1)
            dve.wait_ge(S["x_loaded"], 16)
            with dve.Fori(0, PAIRS) as i:
                for k in range(2):
                    block_stats(X, i * 2 + k)
            inv_std(1)
            prep = Steps(dve, "prep_step")

            def gates(i):
                c0, width = i * (CH // 8), CH // 8
                at, here = ds(c0, width), dstB[:, ds(c0 + 1, width)]
                v.tensor_tensor(SAME_P[:, at], dstB[:, at], here, ALU.is_equal).then_inc(S["gates_made"], 1)
                v.tensor_tensor(SAME_N[:, at], here, dstB[:, ds(c0 + 2, width)], ALU.is_equal).then_inc(S["gates_made"], 1)
                v.tensor_tensor(is_loop[:, at], srcB[:, at], here, ALU.is_equal).then_inc(S["gates_made"], 1)
                dve.wait_ge(*done("gates_made", i * 5 + 2))
                v.tensor_scalar(ADD_P[:, at], SAME_P[:, at], 1.0, BIG, ALU.subtract, ALU.mult).then_inc(S["gates_made"], 1)
                v.tensor_scalar(ADD_N[:, at], SAME_N[:, at], 1.0, BIG, ALU.subtract, ALU.mult).then_inc(S["gates_made"], 1)

            def count_loops():
                dve.wait_ge(*done("gates_made", 40))
                prep.run(v.tensor_reduce(cols[:, 0:1], SAME_P[:, :], AX.X, ALU.min))
                prep.run(v.tensor_reduce(cols[:, 1:2], SAME_N[:, :], AX.X, ALU.min))
                prep.run(scan(loops, SAME_P[:, :], is_loop[:, :], 0.0, ALU.mult, ALU.add))

            def first_loops():
                dve.wait_ge(*done("xc_row", 1))
                prep.run(v.tensor_copy(grow[:, 0:2, :].rearrange("a b n -> a (b n)"), PS[7][0:1, 0:2 * P]))
                dve.sem_inc(S["xc_col"], 1)
                prep.run(v.tensor_scalar(grow[:, 2:4, :], grow[:, 0:2, :], 1.0, BIG, ALU.subtract, ALU.mult))
                prep.run(exchange(True, 0, ALU.mult, ALU.add))
                prep.run(scan(loops, SAME_P[:, :], is_loop[:, :], cols[:, 2:3], ALU.mult, ALU.add))
                prep.run(v.scalar_tensor_tensor(LOOP1[:, :], loops, 1.0, is_loop[:, :], ALU.is_equal, ALU.mult))

            for l in range(2):
                soft = Steps(dve, "soft_step")
                soft.base = SOFT * l
                def normal(n, k):
                    dve.wait_ge(*done("tp_ready", n + (2 * NB * l - 1)))
                    if l:
                        dve.wait_ge(*done("x_kept", n - 1))
                    normalise(xn[k], X, n).then_inc(S["xn_ready"], 1)

                def queries(n, k):
                    at = ds(n * P, P)
                    dve.wait_ge(*done("proj_ready", n + (NB * l + 1)))
                    if l:
                        dve.wait_ge(*done("x_kept", n + 1))
                        v.tensor_tensor(Y[:, at], PS[2 + k][:, 3 * D:4 * D], X[:, at], ALU.add).then_inc(S["batch_step"], 1)
                    v.tensor_scalar(QT[:, at], PS[2 + k][:, 0:D], 0.25, None, ALU.mult).then_inc(S["q_made"], 1)

                pipelined(dve, (normal, 3), (queries, 0))
                if l:
                    dve.wait_ge(*done("batch_step", NB))
                    dve.wait_ge(*done("x_kept", NB))
                dve.wait_ge(S["rel_stored"], 32)
                def logits(i, s):
                    dve.wait_ge(rel_loaded[s], i * 16 + 16 * (PAIRS * l + 1))
                    for hh in range(2):
                        dve.wait_ge(*done("qe_ready", i * 8 + (8 * PAIRS * l + 4 * s + 2 * hh - 2)))
                        for nf in range(2):
                            v.tensor_scalar(OHT[:, hh, nf, :], REL[:, s, hh * 8 * P:(hh + 1) * 8 * P], iota_part[:, nf:nf + 1], None,
                                            ALU.is_equal).then_inc(S["oht_ready"], 1)
                    def add_products(q4):
                        dve.wait_ge(*done("prod_done", i * 8 + (8 * PAIRS * l + 4 * s + q4 + 1)))
                        if q4 == 0:
                            dve.wait_ge(*done("lt_ready", i * 2 + (NB * l + s - 1)))
                        v.tensor_reduce(Ls[s].rearrange("p (h j) -> p j h", h=H)[:, 4 * q4:4 * q4 + 4, :],
                                        prod[q4].rearrange("p (j h c) -> p j h c", j=4, h=H), AX.X, ALU.add).then_inc(S["l_ready"], 1)

                    for q4 in range(4):
                        kk = KV[:, s, 4 * q4:4 * q4 + 4, 0:D]
                        if q4 % 2 == 0:
                            dve.wait_ge(gathered[s][q4 // 2], i * 128 + 128 * (PAIRS * l + 1))
                        if l:
                            dve.wait_ge(*done("e_ready", i * 8 + (4 * s + q4 + 1)))
                            ep = PS[4 + q4 % 2][:, :].rearrange("p (j d) -> p j d", j=4)
                            vv = KV[:, s, 4 * q4:4 * q4 + 4, D:2 * D]
                            v.tensor_tensor(kk, kk, ep, ALU.add).then_inc(S["batch_step"], 1)
                            v.tensor_tensor(vv, vv, ep, ALU.add).then_inc(S["e_used"], 1)
                            dve.wait_ge(*done("batch_step", i * 8 + (NB + 4 * s + q4 + 1)))
                        dve.wait_ge(*done("qe_ready", i * 8 + (8 * PAIRS * l + 4 * s + q4 + 1)))
                        dve.wait_ge(*done("l_ready", i * 8 + (8 * PAIRS * l + 4 * s + q4 - 3)))
                        v.tensor_tensor(prod[q4].rearrange("p (j d) -> p j d", j=4), kk, PS[q4][:, :].rearrange("p (j d) -> p j d", j=4),
                                        ALU.mult).then_inc(S["prod_done"], 1)
                        if q4:
                            add_products(q4 - 1)
                    add_products(3)

                def batches(first, end, also=None):
                    with dve.Fori(first, end) as i:
                        for s in range(2):
                            logits(i, s)
                        if also:
                            also(i)

                if l == 0:
                    dve.wait_ge(S["chunks_loaded"], 16 * 2 * H)
                    batches(0, 8, gates)
                    count_loops()
                    batches(8, 10)
                    first_loops()
                    batches(10, PAIRS)
                else:
                    batches(0, PAIRS)
                dve.wait_ge(*done("lb_ready", NB * (l + 1)))
                dve.sem_inc(S["logits_done"], 1)
                F1 = FB[:, :]
                scan(F1, ADD_P[:, :], LB[:, :], -BIG, ALU.add, ALU.max).then_inc(S["xc_col"], 1)
                rev = lambda x: x[:, ::-1]
                soft.run(exchange(True, 2, ALU.add, ALU.max))
                soft.run(scan(F1, ADD_P[:, :], LB[:, :], cols[:, 2:3], ALU.add, ALU.max))
                scan(rev(MB[:, :]), rev(ADD_N[:, :]), rev(F1), -BIG, ALU.add, ALU.max).then_inc(S["xc_col"], 1)
                soft.run(exchange(False, 3, ALU.add, ALU.max))
                soft.run(scan(rev(MB[:, :]), rev(ADD_N[:, :]), rev(F1), cols[:, 2:3], ALU.add, ALU.max))
                v.tensor_tensor(LB[:, :], LB[:, :], MB[:, :], ALU.subtract).then_inc(S["shifted"], 1)
                dve.wait_ge(*done("exp_ready", l + 1))
                if l == 0:
                    soft.run(v.scalar_tensor_tensor(LB[:, :], LOOP1[:, :], 1.0, LB[:, :], ALU.add, ALU.mult))
                else:
                    dve.sem_inc(S["soft_step"], 1)
                    soft.n += 1
                scan(F1, SAME_P[:, :], LB[:, :], 0.0, ALU.mult, ALU.add).then_inc(S["xc_col"], 1)
                soft.run(exchange(True, 0, ALU.mult, ALU.add))
                soft.run(scan(F1, SAME_P[:, :], LB[:, :], cols[:, 2:3], ALU.mult, ALU.add))
                scan(rev(MB[:, :]), rev(SAME_N[:, :]), rev(F1), 0.0, ALU.mult, ALU.max).then_inc(S["xc_col"], 1)
                soft.run(exchange(False, 1, ALU.mult, ALU.max))
                soft.run(scan(rev(MB[:, :]), rev(SAME_N[:, :]), rev(F1), cols[:, 2:3], ALU.mult, ALU.max))
                soft.run(v.reciprocal(MB[:, :], MB[:, :]))
                soft.run(v.tensor_tensor(LB[:, :], LB[:, :], MB[:, :], ALU.mult))
                assert soft.n == SOFT
                dve.wait_ge(*done("aet_used", 7 * (l + 1)))
                dve.wait_ge(*done("agg_zeroed", 3 * (l + 1)))

                def one_hots(i, q):
                    for st in range(2):
                        u = 2 * st + q
                        dve.wait_ge(*done(f"sum{st}_ready", i * 8 + (64 * l + 4 * q - 4)))
                        v.tensor_tensor(OH4[u].rearrange("p (m n) -> p m n", m=HALF),
                                        iota_row[:, :].unsqueeze(1).broadcast_to([P, HALF, P]),
                                        rel_edge[:, ds(i * G + (st * 8 * G + q * HALF), HALF)].unsqueeze(2).broadcast_to([P, HALF, P]),
                                        ALU.is_equal).then_inc(oh_ready[u], 1)

                def add_up(i, q):
                    for m in range(HALF):
                        n = q * HALF + m
                        if m % 4 == 0:
                            firsts = values(first_row, i * 32 + (16 * J + q * 16 + m), min(4, HALF - m), ENG.DVE, N)
                            dve.wait_ge(*done("sum1_ready", i * 8 + (l * 64 + q * 4 + m // 4 + 1)))
                        dve.wait_ge(*done("sum1_added", i * G + (l * 8 * G + n - 1)))
                        at = AGG[1 + n % 2][:, ds(firsts[m % 4], P)]
                        v.tensor_tensor(at, at, PS[4 + m // 4][:, m % 4 * P:(m % 4 + 1) * P], ALU.add).then_inc(S["sum1_added"], 1)

                last = J // 2 - 1
                one_hots(0, 0)
                with dve.Fori(0, last) as i:
                    one_hots(i, 1)
                    add_up(i, 0)
                    one_hots(i + 1, 0)
                    add_up(i, 1)
                one_hots(last, 1)
                add_up(last, 0)
                add_up(last, 1)
                dve.wait_ge(*done("act_col", 16 * G * (l + 1)))
                dve.wait_ge(*done("sum1_added", 8 * G * (l + 1)))
                def add_streams(n, k):
                    at = ds(n * P, P)
                    dve.wait_ge(*done("att_ready", n + (NB * l - 1)))
                    v.tensor_tensor(xn[k], QT[:, at], AG1[:, at], ALU.add).then_inc(S["half_sum"], 1)

                def add_last_stream(n, k):
                    dve.wait_ge(*done("half_sum", n + (NB * l + 1)))
                    v.tensor_tensor(xn[k], xn[k], AG2[:, ds(n * P, P)], ALU.add).then_inc(S["sum_ready"], 1)

                def residual(n, k):
                    at = ds(n * P, P)
                    dve.wait_ge(*done("att_ready", n + (NB * l + 1)))
                    v.tensor_tensor(Y[:, at], PS[k][:, 0:P], (Y if l else X)[:, at], ALU.add).then_inc(S["res_ready"], 1)

                def residual_stats(n, k):
                    dve.wait_ge(*done("res_ready", n + (NB * l + 1)))
                    block_stats(Y, n)

                pipelined(dve, (add_streams, 4), (add_last_stream, 3), (residual, 1), (residual_stats, 0))
                inv_std(2 if l == 0 else 4)

                def normal2(n, k):
                    if l == 0:
                        dve.wait_ge(*done("tp_ready", n + (NB - 1)))
                    else:
                        dve.wait_ge(*done("ln_affine", n * 3 - 5))
                    normalise(xn[k], Y, n).then_inc(S["xn_ready"], 1)

                def turned2(n, k):
                    dve.wait_ge(*done("tp_ready", n + ((2 * l + 1) * NB + 1)))
                    dve.wait_ge(*done("hidden_ready", n + (NB * l - 1)))
                    if l == 0:
                        v.tensor_scalar(hT[k], PS[k][:, 0:P], gb[:, 2:3], gb[:, 3:4], ALU.mult, ALU.add).then_inc(S["ht_ready"], 1)
                    else:
                        v.tensor_copy(hT[k], PS[k][:, 0:P]).then_inc(S["ht_ready"], 1)

                def add_ffn(n, k):
                    at = ds(n * P, P)
                    dve.wait_ge(*done("ffn_ready", n + (NB * l + 1)))
                    if l == 0:
                        dve.wait_ge(*done("x_summed", n + 1))
                        v.tensor_tensor(X[:, at], PS[4 + k][:, 0:P], X[:, at], ALU.add).then_inc(S["ffn_added"], 1)
                    else:
                        v.tensor_tensor(Y[:, at], PS[4 + k][:, 0:P], Y[:, at], ALU.add).then_inc(S["ffn_added"], 1)

                def ffn_stats(n, k):
                    dve.wait_ge(*done("ffn_added", n + (NB * l + 1)))
                    block_stats(Y if l else X, n)

                pipelined(dve, (normal2, 4), (turned2, 3), (add_ffn, 1), (ffn_stats, 0))
                inv_std(3 if l == 0 else 5)

            def normal3(n, k):
                dve.wait_ge(*done("ln_last", n * 2 - 3))
                normalise(xn[k], Y, n).then_inc(S["xn_ready"], 1)

            def add_input(n, k):
                at = ds(n * P, P)
                dve.wait_ge(*done("ln_last", n * 2 + 2))
                v.tensor_tensor(X[:, at], X[:, at], hN[k], ALU.add).then_inc(S["x_out"], 1)

            def out_stats(n, k):
                dve.wait_ge(*done("x_out", n + 1))
                block_stats(X, n)

            pipelined(dve, (normal3, 3), (add_input, 1), (out_stats, 0))
            inv_std(6)
            with dve.Fori(0, PAIRS) as i:
                for k in range(2):
                    normalise(Y[:, ds(i * (2 * P) + k * P, P)], X, i * 2 + k).then_inc(S["out_made"], 1)


SOFT = 11
FIRST_WEIGHTS = 17
WEIGHTS = 22

_SHAPED = ["L0_gnn_Wq", "L0_gnn_bq", "L0_gnn_Wk", "L0_gnn_bk", "L0_gnn_Wv", "L0_gnn_bv", "L0_gnn_Wo", "L0_gnn_bo",
           "L0_gnn_g1", "L0_gnn_b1", "L0_gnn_g2", "L0_gnn_b2", "L0_gnn_W1", "L0_gnn_bf1", "L0_gnn_W2", "L0_gnn_bf2",
           "L1_gnn_Wq", "L1_gnn_bq", "L1_gnn_Wk", "L1_gnn_bk", "L1_gnn_Wv", "L1_gnn_bv", "L1_gnn_We", "L1_gnn_Wskip",
           "L1_gnn_bskip", "L1_gnn_g1", "L1_gnn_b1", "L1_gnn_g2", "L1_gnn_b2", "L1_gnn_Wf1", "L1_gnn_bf1",
           "L1_gnn_Wf2", "L1_gnn_bf2"]


def kernel(**inputs):
    import numpy as np
    import concourse.bacc as bacc
    from concourse.bass_utils import run_bass_kernel_spmd as run

    nc = bacc.Bacc("TRN2", target_bir_lowering=False, num_devices=1)
    src = np.zeros(EP, np.int32)
    src[:E] = inputs["src"]
    dst = np.full(EP + 2, N, np.int32)
    dst[0] = -1
    dst[EP + 1] = N + 1
    dst[1:E + 1] = inputs["dst"]
    x = np.zeros((NP, D), np.float32)
    x[:N] = inputs["x"]
    edges = np.zeros((EP, ED), np.float32)
    edges[:E] = inputs["edge_attr_64"]
    arrays = {
        "x": x,
        "src": src,
        "dst": dst,
        "src_batch": np.ascontiguousarray(src.reshape(J, G, P).transpose(1, 2, 0)),
        "dst_edge": np.ascontiguousarray(dst[1:EP + 1].reshape(T, P).T),
        "dst_first": np.ascontiguousarray(dst[1:EP + 1].reshape(T, P)[:, 0]),
        "edge_batch": np.ascontiguousarray(edges.reshape(J, G, P, ED).transpose(1, 3, 0, 2)).reshape(G, ED, J * P),
    }
    for name in _SHAPED:
        arrays[name] = np.ascontiguousarray(inputs[name])
    units = np.full((2 * J, 16), N, np.int32)
    units[:, :HALF] = arrays["dst_first"].reshape(2 * J, HALF)
    arrays["dst_units"] = units.reshape(-1)
    a = {}
    for name, v in arrays.items():
        dt = U32 if name == "src_batch" else mybir.dt.from_np(v.dtype)
        a[name] = nc.dram_tensor(f"in_{name}", v.shape, dt, kind="ExternalInput").ap()
    out = nc.dram_tensor("out_0", (N, D), F32, kind="ExternalOutput").ap()
    build(nc, a, out)
    r = run(nc, [{f"in_{k}": v for k, v in arrays.items()}], core_ids=[0])
    return r.results[0]["out_0"]
```

```python
from contextlib import ExitStack

import concourse.bass as bass
from concourse import mybir

F32 = mybir.dt.float32
BF16 = mybir.dt.bfloat16
I32 = mybir.dt.int32
U32 = mybir.dt.uint32
U8 = mybir.dt.uint8
ACT = mybir.ActivationFunctionType
ALU = mybir.AluOpType
AX = mybir.AxisListType
ENG = mybir.EngineType
ds = bass.ds

P = 128
N = 3125
E = 53125
D = 128
H = 8
C = D // H
FF = 512
ED = 64
NB = 26
NP = NB * P
PAIRS = NB // 2
J = 16
G = 26
T = J * G
EP = T * P
CH = G * P
HALF = G // 2
UNIT = HALF * P
BW = 10 * D
BIG = 3e38
HALF_BATCH = 8 * 16
START = 32
EPS = 1e-5


def build(nc, a, out):
    kv_table = nc.dram_tensor("kv_table", (NP, 2 * D), F32, kind="Internal").ap()
    v_edges = nc.dram_tensor("v_edges", (P, T * D), F32, kind="Internal").ap()
    rel_dram = nc.dram_tensor("rel_dram", (G, J * P), BF16, kind="Internal").ap()
    block_dram = nc.dram_tensor("block_dram", (G, J), I32, kind="Internal").ap()

    with ExitStack() as ctx:
        def sb(name, shape, dt=F32):
            return ctx.enter_context(nc.sbuf_tensor(name, shape, dt))

        def sem(name):
            return ctx.enter_context(nc.semaphore(name))

        X = sb("X", [P, NP])
        Y = sb("Y", [P, NP])
        QT = sb("QT", [P, NP + P])
        AG1 = sb("AG1", [P, NP + P])
        KV = sb("KV", [P, 2, J, 2 * D])
        OHT = sb("OHT", [P, 2, 2, 8 * P])
        REL = sb("REL", [P, 2, J * P], BF16)
        LB = sb("LB", [P, CH])
        FB = sb("FB", [P, CH])
        MB = sb("MB", [P, CH])
        AE = MB
        ADD_P = sb("ADD_P", [P, CH], BF16)
        ADD_N = sb("ADD_N", [P, CH], BF16)
        SAME_P = sb("SAME_P", [P, CH], U8)
        SAME_N = sb("SAME_N", [P, CH], U8)
        LOOP1 = sb("LOOP1", [P, CH], U8)
        idx = sb("idx", [P, 2, J], U32)
        dst_first = sb("dst_first", [P, T], I32)
        rel_edge = sb("rel_edge", [P, T])
        block_row = sb("block_row", [1, T], I32)
        first_row = sb("first_row", [1, 2 * J * 16], I32)
        iota_row = sb("iota_row", [P, P])
        iota_part = sb("iota_part", [P, 2])
        minus_part = sb("minus_part", [P, 2])
        one_col = sb("one_col", [P, 1])
        ident = sb("ident", [P, P])
        ones = sb("ones", [1, P])
        ones3 = sb("ones3", [3, P], BF16)
        Wp = [sb("Wp0", [P, 3 * D]), sb("Wp1", [P, 4 * D])]
        BIAS = sb("BIAS", [3, BW], BF16)
        Bp = [BIAS[:, 0:3 * D], BIAS[:, 3 * D:7 * D]]
        bo = BIAS[:, 7 * D:8 * D]
        bf2 = [BIAS[:, (8 + l) * D:(9 + l) * D] for l in range(2)]
        Wo = sb("Wo", [P, D])
        We = sb("We", [ED, D])
        W1 = [sb(f"W1{l}", [P, FF]) for l in range(2)]
        W2 = [sb(f"W2{l}", [P, 4, D]) for l in range(2)]
        bf1 = [sb(f"bf1{l}", [P, 4]) for l in range(2)]
        gb = sb("gb", [P, 4])
        GB = sb("GB", [P, 4, D])
        MEAN = sb("MEAN", [P, NB])
        RS = sb("RS", [P, NB])
        SD = sb("SD", [P, NB])
        BN = sb("BN", [P, NB, 6])
        cols = sb("cols", [P, 4])
        grow = sb("grow", [1, 4, P])
        srow = sb("srow", [1, 2, P + 2])
        TMP = sb("TMP", [P, 1280])

        PS = [ctx.enter_context(nc.psum_tensor(f"PS{b}", [P, 512], F32)) for b in range(8)]

        xn = [TMP[:, k * D:(k + 1) * D] for k in range(2)]
        hN = [TMP[:, 256 + k * D:256 + (k + 1) * D] for k in range(2)]
        hT = [TMP[:, 512 + k * P:512 + (k + 1) * P] for k in range(2)]
        kv_out = [KV[:, 0, k, :] for k in range(4)]
        gT = [KV[:, 1, 2 * k:2 * k + 2, :].rearrange("p a (b n) -> p (a b) n", b=2) for k in range(2)]
        bias_raw = FB[0:3, 2048:2048 + BW]
        bias_hi = MB[0:3, 0:BW // 2].bitcast(BF16)
        bias_mid = MB[0:3, BW // 2:BW].bitcast(BF16)
        bias_lo = MB[0:3, BW:3 * BW // 2].bitcast(BF16)
        bias_rest = MB[0:3, 3 * BW // 2:5 * BW // 2]
        AG2 = OHT[:, :, :, :].rearrange("p a b n -> p (a b n)")[:, 0:NP + P]
        AGG = [QT, AG1, AG2]
        prod = [FB[:, r * 512:(r + 1) * 512] for r in range(4)]
        Ls = [TMP[:, 1024 + s * P:1024 + (s + 1) * P] for s in range(2)]
        ea = [AG1[0:ED, hh * 8 * P:(hh + 1) * 8 * P] for hh in range(2)]
        kv_flat = KV[:, :, :, :].rearrange("p s j d -> p (s j d)")
        dstB = AG1[:, 0:CH + 2].bitcast(I32)
        srcB = Y[:, 0:CH].bitcast(I32)
        is_loop = MB
        loops = Y[:, 0:CH]
        V4 = [kv_flat[:, u * UNIT:(u + 1) * UNIT] for u in range(4)]
        OH4 = [LB[:, 0:UNIT], LB[:, UNIT:2 * UNIT], FB[:, 0:UNIT], FB[:, UNIT:2 * UNIT]]
        ae4 = AE[:, :].rearrange("p (g h j) -> p g h j", g=G, h=H)
        dstG = OHT[0:G, 0, :, :].rearrange("p a n -> p (a n)").bitcast(I32)
        relG = REL[0:G, 0, :]
        blkG = OHT[0:G, 1, 0, 0:J].bitcast(I32)
        dst_edge = OHT[:, 1, 1, 0:T].bitcast(I32)

        S = {n: sem(n) for n in """x_loaded dstg_loaded dste_loaded chunks_loaded first_weights weights_loaded
            rel_stored block_loaded out_stored""".split()}
        counts = """consts_made rel_made prep_step kv_copied kv_free v_free gates_made
            pool_go sp_go stat_step moment_step var_ready sd_ready rs_ready
            xn_ready tp_ready ht_ready proj_ready q_made x_kept
            ln_affine ln_last half_sum sum_ready att_ready res_ready hidden_ready gelu_ready ffn_ready ffn_added
            shift_made out_made out2_made bias_made bias_step warmed x_summed x_shifted x_out
            oht_ready oht2_step oht2_ready qe_ready prod_done e_ready e_used l_ready lt_ready lb_ready logits_done batch_step
            xc_col xc_row xc_scanned xc_back soft_step shifted exp_ready inverse_step aet_ready aet_used
            agg_zeroed sum0_ready sum1_ready sum1_added act_col
            """.split()
        S.update((n, sem(n)) for n in counts)

        def values(row, at, n, engine, most):
            return nc.values_load_multi_w_load_instructions(row[0:1, ds(at, n)], engines=(engine,), min_val=0, max_val=most,
                                                               skip_runtime_bounds_check_because="they come from dst, which holds indices of nodes")[1]

        def pipelined(eng, *stages, slots=2, unroll=4):
            top = max(ahead for f, ahead in stages)

            def step(n, first, k):
                for f, ahead in stages:
                    if first is None or 0 <= first + ahead < NB:
                        f(n + ahead, (k + ahead) % slots)

            for n in range(-top, 0):
                step(n, n, n)
            trips = (NB - top) // unroll
            with eng.Fori(0, trips) as i:
                for k in range(unroll):
                    step(i * unroll + k, None, k)
            for n in range(unroll * trips, NB):
                step(n, n, n)

        def blocks(eng, f, first=0, end=NB, unroll=4):
            trips = (end - first) // unroll
            with eng.Fori(0, trips) as i:
                for k in range(unroll):
                    f(i * unroll + (first + k), (first + k) % 2)
            for n in range(first + unroll * trips, end):
                f(n, n % 2)

        def done(name, n):
            return S[name], n + START

        kv_stored = [sem(f"kv_stored{k}") for k in range(4)]
        kv_uses = [len(range(k, NB, 4)) for k in range(4)]
        idx_loaded = [sem(f"idx_loaded{s}") for s in range(2)]
        rel_loaded = [sem(f"rel_loaded{s}") for s in range(2)]
        ea_loaded = [sem(f"ea_loaded{s}") for s in range(2)]
        gathered = [[sem(f"gathered{s}{hh}") for hh in range(2)] for s in range(2)]
        v_stored = [[sem(f"v_stored{s}{hh}") for hh in range(2)] for s in range(2)]
        v_loaded = [sem(f"v_loaded{u}") for u in range(4)]
        pv_ready = [sem(f"pv_ready{u}") for u in range(4)]
        oh_ready = [sem(f"oh_ready{u}") for u in range(4)]

        class Steps:

            def __init__(self, eng, name):
                self.eng, self.s, self.base, self.n = eng, S[name], 0, 0

            def run(self, ins):
                ins.then_inc(self.s, 1)
                self.n += 1
                self.eng.wait_ge(self.s, self.base + self.n + START)

        block = ctx.enter_context(nc.Block())

        @block.sync
        def _(sp):
            sp.dma_start(X[:, :].rearrange("p (b d) -> p b d", b=NB), a["x"].rearrange("(b p) d -> p b d", p=P)).then_inc(S["x_loaded"], 16)
            sp.dma_start(dstG.rearrange("g (j e) -> g j e", j=J),
                         a["dst"][1:EP + 1].rearrange("(j g e) -> g j e", j=J, g=G)).then_inc(S["dstg_loaded"], 16)
            sp.dma_start(dst_edge, a["dst_edge"]).then_inc(S["dste_loaded"], 16)
            sp.dma_start(dst_first[:, :], a["dst_first"].rearrange("(a t) -> a t", a=1).broadcast_to([P, T])).then_inc(S["dste_loaded"], 16)
            row = lambda v: v.rearrange("(a n) -> a n", a=1)
            biases = ["L0_gnn_bq", "L0_gnn_bk", "L0_gnn_bv", "L1_gnn_bq", "L1_gnn_bk", "L1_gnn_bv", "L1_gnn_bskip", "L0_gnn_bo",
                      "L0_gnn_bf2", "L1_gnn_bf2"]
            for n, name in enumerate(biases):
                sp.dma_start(bias_raw[:, n * D:(n + 1) * D], row(a[name]).broadcast_to([3, D])).then_inc(S["first_weights"], 16)

            sp.wait_ge(*done("rel_made", 2))
            sp.dma_start(rel_dram, relG).then_inc(S["rel_stored"], 16)
            sp.dma_start(block_dram, blkG).then_inc(S["rel_stored"], 16)
            sp.wait_ge(S["rel_stored"], 32)
            sp.dma_start(first_row[:, :], a["dst_units"].rearrange("(a n) -> a n", a=1)).then_inc(S["block_loaded"], 16)
            for h in range(H):
                sp.dma_start(dstB[h * J:(h + 1) * J, :],
                             bass.AP(a["dst"].tensor, 0, [[CH, J], [1, CH + 2]])).then_inc(S["chunks_loaded"], 16)
                sp.dma_start(srcB[h * J:(h + 1) * J, :],
                             a["src"].rearrange("(j n) -> j n", j=J)).then_inc(S["chunks_loaded"], 16)
            sp.dma_start(block_row[:, :], block_dram.rearrange("g j -> (g j)").rearrange("(a n) -> a n", a=1)).then_inc(S["block_loaded"], 16)

            for l in range(2):
                def store(n, k):
                    sp.wait_ge(*done("kv_copied", n + (l * NB + 1)))
                    sp.sem_inc(S["sp_go"], 1)
                    sp.dma_start(kv_table[ds(n * P, P), :], kv_out[k]).then_inc(kv_stored[k], 16)

                def stored(n, k):
                    sp.wait_ge(kv_stored[k], n * 4 + (16 - 4 * k + 16 * kv_uses[k] * l))
                    sp.sem_inc(S["kv_free"], 1)

                pipelined(sp, (store, 2), (stored, 0), slots=4)
                def indices(n, s, first=False):
                    if not first:
                        sp.wait_ge(gathered[s][1], n * 64 + (HALF_BATCH * PAIRS * l - 64 * s))
                    sp.sem_inc(S["sp_go"], 1)
                    sp.dma_start(idx[:, s, :], a["src_batch"][ds(n, 1), :, :].rearrange("a p j -> (a p) j")).then_inc(idx_loaded[s], 16)
                    sp.wait_ge(*done("oht_ready", n * 2 + (4 * PAIRS * l - 2)))
                    sp.wait_ge(*done("oht2_ready", n * 2 + (4 * PAIRS * l - 2)))
                    sp.sem_inc(S["sp_go"], 1)
                    sp.dma_start(REL[:, s, :], rel_dram[ds(n, 1), :].broadcast_to([P, J * P])).then_inc(rel_loaded[s], 16)

                def features(n, s):
                    for hh in range(2):
                        sp.wait_ge(*done("e_ready", n * 4 + (2 * hh - 2)))
                        sp.sem_inc(S["sp_go"], 1)
                        sp.dma_start(ea[hh], a["edge_batch"][ds(n, 1), :, hh * 8 * P:(hh + 1) * 8 * P]
                                     .rearrange("a p j -> (a p) j")).then_inc(ea_loaded[hh], 16)

                if l == 0:
                    indices(0, 0, first=True)
                    indices(1, 1, first=True)
                    with sp.Fori(1, PAIRS) as i:
                        for s in range(2):
                            indices(i * 2 + s, s)
                else:
                    pipelined(sp, (indices, 1), (features, 0), unroll=2)
                for s in range(2):
                    for hh in range(2):
                        sp.wait_ge(v_stored[s][hh], 16 * PAIRS * (l + 1))
                    sp.wait_ge(*done("logits_done", l + 1))
                with sp.Fori(0, J // 2) as i:
                    for q in range(2):
                        for st in (1, 0):
                            u = 2 * st + q
                            sp.wait_ge(*done(f"sum{st}_ready", i * 8 + (64 * l + 4 * q - 4)))
                            sp.sem_inc(S["sp_go"], 1)
                            sp.dma_start(V4[u], v_edges[:, ds(i * (G * P) + (st * (J // 2) * G + q * HALF) * P, UNIT)]).then_inc(v_loaded[u], 16)
            full = N // P
            for b0, b1 in ((0, DVE_OUT // 2), (DVE_OUT, (DVE_OUT + full) // 2), (DVE_OUT // 2, DVE_OUT), ((DVE_OUT + full) // 2, full)):
                if b1 <= DVE_OUT:
                    sp.wait_ge(*done("out_made", b1))
                else:
                    sp.wait_ge(*done("out2_made", (NB if b1 == full else b1) - DVE_OUT))
                sp.dma_start(out[b0 * P:b1 * P, :].rearrange("(b p) d -> p b d", p=P),
                             Y[:, b0 * P:b1 * P].rearrange("p (b d) -> p b d", b=b1 - b0)).then_inc(S["out_stored"], 16)
            sp.dma_start(out[full * P:N, :], Y[0:N - full * P, full * P:(full + 1) * P]).then_inc(S["out_stored"], 16)
            sp.wait_ge(S["out_stored"], 80)

        @block.gpsimd
        def _(pool):
            g = nc.gpsimd
            g.memset(ones[:, :], 1.0).then_inc(S["consts_made"], 1)
            g.memset(ones3[:, :], 1.0).then_inc(S["consts_made"], 1)
            g.memset(one_col[:, :], 1.0).then_inc(S["consts_made"], 1)
            g.memset(ident[:, :], 0.0).then_inc(S["consts_made"], 1)
            g.memset(srow[:, :, :], 0.0).then_inc(S["consts_made"], 1)
            g.memset(QT[:, NP:NP + P], 0.0).then_inc(S["consts_made"], 1)
            pool.wait_ge(*done("consts_made", 6))
            g.affine_select(out=ident[:, :], in_=ident[:, :], compare_op=ALU.not_equal, fill=1.0,
                            base=0, pattern=[[-1, P]], channel_multiplier=1).then_inc(S["consts_made"], 1)
            g.iota(iota_row[:, :], pattern=[[1, P]], base=0, channel_multiplier=0,
                   allow_small_or_imprecise_dtypes=True).then_inc(S["consts_made"], 1)
            g.iota(minus_part[:, :], pattern=[[-P, 2]], base=0, channel_multiplier=-1,
                   allow_small_or_imprecise_dtypes=True).then_inc(S["consts_made"], 1)
            g.iota(iota_part[:, :], pattern=[[P, 2]], base=0, channel_multiplier=1,
                   allow_small_or_imprecise_dtypes=True).then_inc(S["consts_made"], 1)

            pool.wait_ge(S["weights_loaded"], 16 * WEIGHTS)
            for l in range(2):
                if l:
                    def keep(n, k):
                        pool.wait_ge(*done("xn_ready", n + (2 * NB + 1)))
                        pool.sem_inc(S["pool_go"], 1)
                        g.tensor_copy(X[:, ds(n * P, P)], xn[k]).then_inc(S["x_kept"], 1)

                    blocks(pool, keep)
                for k in range(4):
                    pool.wait_ge(kv_stored[k], 16 * kv_uses[k] * (l + 1))
                with pool.Fori(0, PAIRS) as i:
                    for s in range(2):
                        pool.wait_ge(idx_loaded[s], i * 16 + 16 * (PAIRS * l + 1))
                        for hh in range(2):
                            pool.wait_ge(*done("l_ready", i * 8 + (8 * PAIRS * l + 4 * s + 2 * hh - 6)))
                            pool.wait_ge(*done("v_free", i * 4 + (2 * NB * l + 2 * s + hh - 3)))
                            pool.sem_inc(S["pool_go"], 1)
                            for j in range(hh * 8, hh * 8 + 8):
                                g.indirect_dma_start(KV[:, s, j, :], None, kv_table,
                                                     bass.IndirectOffsetOnAxis(ap=idx[:, s, j:j + 1], axis=0)).then_inc(gathered[s][hh], 16)
                pool.wait_ge(*done("logits_done", l + 1))
                for sums in AGG:
                    g.memset(sums[:, :], 0.0).then_inc(S["agg_zeroed"], 1)
                if l:
                    x3 = X[:, :].rearrange("p (n d) -> p n d", n=NB)
                    g.tensor_tensor(x3, x3, GB[:, 3, :].unsqueeze(1).broadcast_to([P, NB, D]), ALU.add).then_inc(S["x_shifted"], 1)
                with pool.Fori(0, J // 2) as i:
                    for q in range(2):
                        pool.wait_ge(*done("aet_used", 7 * l + (7 if q else 4)))
                        for st in (1, 0):
                            u = 2 * st + q
                            pool.wait_ge(v_loaded[u], i * 16 + 16 * (l * 8 + 1))
                            pool.sem_inc(S["pool_go"], 1)
                            v4 = V4[u].rearrange("p (m h c) -> p m h c", m=HALF, h=H)
                            at = ae4[:, q * HALF:(q + 1) * HALF, :, ds(i + 8 * st, 1)].broadcast_to([P, HALF, H, C])
                            g.tensor_tensor(v4, v4, at, ALU.mult).then_inc(pv_ready[u], 1)
                pool.wait_ge(*done("sum1_added", 8 * G * (l + 1)))
                def join(n, k):
                    at = ds(n * P, P)
                    g.tensor_tensor(AG1[:, at], AG1[:, at], AG2[:, at], ALU.add).then_inc(S["half_sum"], 1)

                blocks(pool, join)
                if l == 0:
                    def sum_residuals(n, k):
                        pool.wait_ge(*done("res_ready", n + 1))
                        at = ds(n * P, P)
                        pool.sem_inc(S["pool_go"], 1)
                        g.tensor_tensor(X[:, at], X[:, at], Y[:, at], ALU.add).then_inc(S["x_summed"], 1)

                    blocks(pool, sum_residuals)
                else:
                    def affine(n, k):
                        at = ds(n * P, P)
                        pool.wait_ge(*done("xn_ready", n + (3 * NB + 1)))
                        pool.sem_inc(S["pool_go"], 1)
                        g.tensor_tensor(Y[:, at], Y[:, at], GB[:, 0, :], ALU.mult).then_inc(S["ln_affine"], 1)
                        pool.wait_ge(*done("ln_affine", n * 3 + 1))
                        pool.wait_ge(*done("tp_ready", n + (3 * NB - 1)))
                        pool.sem_inc(S["pool_go"], 1)
                        g.tensor_tensor(hN[k], Y[:, at], GB[:, 1, :], ALU.add).then_inc(S["ln_affine"], 1)
                        pool.wait_ge(*done("ln_affine", n * 3 + 2))
                        pool.sem_inc(S["pool_go"], 1)
                        g.tensor_tensor(Y[:, at], Y[:, at], GB[:, 1, :], ALU.add).then_inc(S["ln_affine"], 1)

                    blocks(pool, affine)

                    def scale_last(n, k):
                        pool.wait_ge(*done("xn_ready", n + (4 * NB + 1)))
                        pool.wait_ge(*done("x_out", n - 1))
                        g.tensor_tensor(hN[k], xn[k], GB[:, 2, :], ALU.mult).then_inc(S["ln_last"], 1)

                    blocks(pool, scale_last)

        @block.scalar
        def _(act):
            sc = nc.scalar

            warmed = Steps(act, "warmed")

            def warm(function):
                warmed.run(sc.activation(cols[0:1, 3:4], ones[0:1, 0:1], function))

            def roots(n):
                warm(ACT.Sqrt)
                act.wait_ge(*done("var_ready", n))
                sc.activation(SD[:, :], RS[:, :], ACT.Sqrt).then_inc(S["sd_ready"], 1)

            def w(dst, src, name="weights_loaded"):
                act.dma_start(dst, src).then_inc(S[name], 16)

            row = lambda v: v.rearrange("(a n) -> a n", a=1)
            col = lambda v: v.rearrange("(n a) -> n a", a=1)
            for n, q in enumerate(("q", "k", "v")):
                w(Wp[0][:, n * D:(n + 1) * D], a[f"L0_gnn_W{q}"], "first_weights")
            for n, v in enumerate(("g1", "b1", "g2", "b2")):
                w(gb[:, n:n + 1], col(a[f"L0_gnn_{v}"]), "first_weights")
            for n, q in enumerate(("q", "k", "v", "skip")):
                w(Wp[1][:, n * D:(n + 1) * D], a[f"L1_gnn_W{q}"])
            w(Wo[:, :], a["L0_gnn_Wo"])
            w(We[:, :], a["L1_gnn_We"])
            for l, f in ((0, ""), (1, "f")):
                w(W1[l][:, :], a[f"L{l}_gnn_W{f}1"])
                w(W2[l][:, :, :], a[f"L{l}_gnn_W{f}2"].rearrange("(c k) n -> k c n", k=P))
                for c in range(4):
                    w(bf1[l][:, c:c + 1], col(a[f"L{l}_gnn_bf1"][c * P:(c + 1) * P]))
            for n, v in enumerate(("g1", "b1", "g2", "b2")):
                w(GB[:, n, :], row(a[f"L1_gnn_{v}"]).broadcast_to([P, D]))

            act.wait_ge(*done("consts_made", 10))
            act.wait_ge(S["first_weights"], 16 * FIRST_WEIGHTS)
            for l in range(2):
                if l == 0:
                    roots(1)
                def turned(n, k):
                    act.wait_ge(*done("tp_ready", n + (2 * NB * l + 1)))
                    act.wait_ge(*done("proj_ready", n + (NB * l - 1)))
                    if l == 0:
                        sc.activation(hT[k % 2], PS[k % 2][:, 0:P], ACT.Identity, bias=gb[:, 1:2], scale=gb[:, 0:1]).then_inc(S["ht_ready"], 1)
                    else:
                        sc.activation(hT[k % 2], PS[k % 2][:, 0:P], ACT.Copy).then_inc(S["ht_ready"], 1)

                def keys_values(n, k):
                    act.wait_ge(*done("q_made", n + (NB * l + 1)))
                    act.wait_ge(*done("kv_free", n + (NB * l - 3)))
                    sc.activation(kv_out[k], PS[2 + k % 2][:, D:3 * D], ACT.Copy).then_inc(S["kv_copied"], 1)

                pipelined(act, (turned, 2), (keys_values, 0), slots=4)
                def one_hots(n, s):
                    act.wait_ge(rel_loaded[s], n * 8 + (16 * PAIRS * l + 16 - 8 * s))
                    act.wait_ge(*done("qe_ready", n * 4 + 8 * PAIRS * l))
                    for nf in range(2):
                        sc.activation(OHT[:, 1, nf, :], REL[:, s, 8 * P:16 * P], ACT.Abs, bias=minus_part[:, nf:nf + 1]).then_inc(S["oht2_step"], 1)
                    for nf in range(2):
                        act.wait_ge(*done("oht2_step", n * 2 + (4 * PAIRS * l + nf + 1)))
                        sc.activation(OHT[:, 1, nf, :], OHT[:, 1, nf, :], ACT.Relu, bias=one_col[:, 0:1], scale=-1.0).then_inc(S["oht2_ready"], 1)

                def batch(n, s, last=False):
                    def free(hh):
                        act.wait_ge(v_stored[s][hh], n * 8 + (16 * PAIRS * l + 16 - 8 * s))
                        act.sem_inc(S["v_free"], 1)

                    for hh in range(2):
                        if l == 0:
                            act.wait_ge(gathered[s][hh], n * 64 + (HALF_BATCH - 64 * s))
                        else:
                            act.wait_ge(*done("e_used", n * 4 + (2 * hh + 2)))
                        act.dma_start(v_edges.rearrange("p (j n) -> p j n", j=J)[:, hh * 8:hh * 8 + 8, ds(n * P, P)],
                                      KV[:, s, hh * 8:hh * 8 + 8, D:2 * D]).then_inc(v_stored[s][hh], 16)
                        if hh == 0:
                            free(0)
                    if not last:
                        one_hots(n + 2, s)
                    free(1)
                    act.wait_ge(*done("lt_ready", n + (NB * l + 1)))
                    sc.activation(LB[:, ds(n * P, P)], PS[6][:, s * P:(s + 1) * P], ACT.Copy).then_inc(S["lb_ready"], 1)

                act.wait_ge(S["rel_stored"], 32)
                act.wait_ge(*done("rel_made", 3))
                one_hots(0, 0)
                one_hots(1, 1)
                with act.Fori(0, PAIRS - 1) as i:
                    for s in range(2):
                        batch(i * 2 + s, s)
                batch(NB - 2, 0, last=True)
                batch(NB - 1, 1, last=True)
                warm(ACT.Exp)
                for p in range(4):
                    act.wait_ge(*done("shifted", 4 * l + p + 1))
                    sc.activation(LB[:, p * QUARTER:(p + 1) * QUARTER], LB[:, p * QUARTER:(p + 1) * QUARTER], ACT.Exp)\
                        .then_inc(S["exp_ready"], 1)
                warm(ACT.Ln)
                act.wait_ge(*done("soft_step", SOFT * l + SUMS - 1))
                right = slice(LEFT * P, CH)
                sc.activation(FB[:, right], MB[:, right], ACT.Ln).then_inc(S["inverse_step"], 1)
                act.wait_ge(*done("inverse_step", 2 * l + 1))
                sc.activation(FB[:, right], FB[:, right], ACT.Exp, scale=-1.0).then_inc(S["inverse_step"], 1)
                for b in range(0, G, 4):
                    act.wait_ge(*done("aet_ready", 7 * l + b // 4 + 1))
                    w_ = min(4, G - b) * P
                    sc.activation(AE[:, b * P:b * P + w_], PS[b // 4 % 4][:, 0:w_], ACT.Copy).then_inc(S["aet_used"], 1)
                act.wait_ge(*done("agg_zeroed", 3 * (l + 1)))
                with act.Fori(0, J // 2) as i:
                    for q in range(2):
                        for m in range(HALF):
                            n = q * HALF + m
                            if m == 0:
                                firsts = values(first_row, i * 32 + q * 16, HALF, ENG.Activation, N)
                            if m % 4 == 0:
                                act.wait_ge(*done("sum0_ready", i * 8 + (l * 64 + q * 4 + m // 4 + 1)))
                            first = firsts[m]
                            p = PS[m // 4][:, m % 4 * P:(m % 4 + 1) * P]
                            act.wait_ge(*done("act_col", i * (2 * G) + (l * 16 * G + 2 * n)))
                            sc.activation(QT[:, ds(first, 1)], p[:, 0:1], ACT.Identity, bias=QT[:, ds(first, 1)]).then_inc(S["act_col"], 1)
                            sc.activation(QT[:, ds(first + 1, P - 1)], p[:, 1:P], ACT.Copy).then_inc(S["act_col"], 1)
                roots(2 if l == 0 else 4)
                def gelus(n, k):
                    act.wait_ge(*done("hidden_ready", n + (NB * l + 1)))
                    act.wait_ge(*done("ffn_ready", n + (NB * l - 1)))
                    for c in range(4):
                        sc.activation(gT[k][:, c, :], PS[2 + k][:, c * P:(c + 1) * P], ACT.Gelu,
                                      bias=bf1[l][:, c:c + 1]).then_inc(S["gelu_ready"], 1)

                act.wait_ge(S["weights_loaded"], 16 * WEIGHTS)
                warm(ACT.Gelu)
                gelus(0, 0)
                gelus(1, 1)
                blocks(act, gelus, first=2)
                roots(3 if l == 0 else 5)
            roots(6)
            act.wait_ge(*done("shift_made", 1))
            act.wait_ge(*done("rs_ready", 6))

            def normalise_last(n, k):
                at, one = ds(n * P, P), ds(n, 1)
                sc.activation(Y[:, at], X[:, at], ACT.Identity, bias=SD[:, one], scale=RS[:, one]).then_inc(S["out2_made"], 1)

            blocks(act, normalise_last, first=DVE_OUT)

        @block.tensor
        def _(pe):
            te = nc.tensor
            for n in counts:
                pe.sem_inc(S[n], START)
            xc = [0]

            def exchange(col, part):
                xc[0] += 1
                pe.wait_ge(*done("xc_col", xc[0]))
                te.matmul(PS[7][0:1, 0:P], col, ident[:, :], start=True, stop=True).then_inc(S["xc_row"], 1)
                pe.wait_ge(*done("xc_scanned", xc[0]))
                te.matmul(PS[7][:, P:P + 1], part, ones[0:1, 0:1], start=True, stop=True).then_inc(S["xc_back"], 1)

            fwd, bwd = srow[0:1, 0, 0:P], srow[0:1, 1, 1:P + 1]

            pe.wait_ge(*done("consts_made", 10))
            pe.wait_ge(S["first_weights"], 16 * FIRST_WEIGHTS)
            pe.wait_ge(*done("bias_made", 1))

            for l in range(2):
                Wd = (3 + l) * D

                def turn(n, k):
                    pe.wait_ge(*done("xn_ready", n + (2 * NB * l + 1)))
                    pe.wait_ge(*done("ht_ready", n + (2 * NB * l - 1)))
                    te.transpose(PS[k][:, 0:P], xn[k], ident[:, :]).then_inc(S["tp_ready"], 1)

                def project(n, k):
                    pe.wait_ge(*done("ht_ready", n + (2 * NB * l + 1)))
                    pe.wait_ge(*done("kv_copied", n + (NB * l - 1)))
                    te.matmul(PS[2 + k][:, 0:Wd], ones3[:, :], Bp[l], start=True, stop=False)
                    te.matmul(PS[2 + k][:, 0:Wd], hT[k], Wp[l][:, :], start=False, stop=True).then_inc(S["proj_ready"], 1)

                pipelined(pe, (turn, 2), (project, 0))
                pe.wait_ge(S["block_loaded"], 32)
                pe.wait_ge(*done("q_made", NB * (l + 1)))
                pe.wait_ge(*done("kv_copied", NB * (l + 1)))
                pe.wait_ge(S["weights_loaded"], 16 * WEIGHTS)
                blks = [None] * 8

                def queries_of(n, s, q4):
                    if q4 % 2 == 0:
                        blks[:] = values(block_row, n * J + 4 * q4, 8, ENG.PE, NP - P)
                        pe.wait_ge(*done("oht2_ready" if q4 // 2 else "oht_ready", n * 2 + (4 * PAIRS * l + 2)))
                    pe.wait_ge(*done("prod_done", n * 4 + (8 * PAIRS * l + q4 - 3)))
                    for jj in range(4):
                        blk = blks[q4 % 2 * 4 + jj]
                        o = PS[q4][:, jj * P:(jj + 1) * P]
                        e0 = ((4 * q4 + jj) % 8) * P
                        te.matmul(o, OHT[:, q4 // 2, 0, e0:e0 + P], QT[:, ds(blk, P)], start=True, stop=False)
                        last = te.matmul(o, OHT[:, q4 // 2, 1, e0:e0 + P], QT[:, ds(blk + P, P)], start=False, stop=True)
                    last.then_inc(S["qe_ready"], 1)

                def edge_part(n, s, q4):
                    if q4 % 2 == 0:
                        pe.wait_ge(ea_loaded[q4 // 2], n * 16 + 16)
                    pe.wait_ge(*done("e_used", n * 4 + (q4 - 1)))
                    for jj in range(4):
                        e0 = ((4 * q4 + jj) % 8) * P
                        last = te.matmul(PS[4 + q4 % 2][:, jj * P:(jj + 1) * P], ea[q4 // 2][:, e0:e0 + P], We[:, :], start=True, stop=True)
                    last.then_inc(S["e_ready"], 1)

                def turn_logits(n, s):
                    pe.wait_ge(*done("l_ready", n * 4 + (8 * PAIRS * l + 4)))
                    pe.wait_ge(*done("lb_ready", n + NB * l))
                    te.transpose(PS[6][:, s * P:(s + 1) * P], Ls[s], ident[:, :]).then_inc(S["lt_ready"], 1)

                def batch(n, s, first=False, last=False):
                    if l:
                        edge_part(n, s, 0)
                        edge_part(n, s, 1)
                    if not first:
                        turn_logits(n - 1, 1 - s)
                    for q4 in range(4):
                        if not last:
                            queries_of(n + 1, 1 - s, q4)
                        if l and q4 < 2:
                            edge_part(n, s, q4 + 2)

                def batches(start, end):
                    with pe.Fori(start, end) as i:
                        for s in range(2):
                            batch(i * 2 + s, s)

                for q4 in range(4):
                    queries_of(0, 0, q4)
                batch(0, 0, first=True)
                batch(1, 1)
                if l == 0:
                    batches(1, 10)
                    pe.wait_ge(*done("prep_step", 3))
                    te.matmul(PS[7][0:1, 0:P], cols[:, 0:1], ident[:, :], start=True, stop=True)
                    te.matmul(PS[7][0:1, P:2 * P], cols[:, 1:2], ident[:, :], start=True, stop=True).then_inc(S["xc_row"], 1)
                    exchange(loops[:, CH - 1:CH], fwd)
                batches(10 if l == 0 else 1, PAIRS - 1)
                batch(NB - 2, 0)
                batch(NB - 1, 1, last=True)
                turn_logits(NB - 1, 1)
                exchange(FB[:, CH - 1:CH], fwd)
                exchange(MB[:, 0:1], bwd)
                exchange(FB[:, CH - 1:CH], fwd)
                exchange(MB[:, 0:1], bwd)
                for b in range(0, G, 4):
                    pe.wait_ge(*done("soft_step", SOFT * l + SUMS + (b // 2 + 2 if b < LEFT else LEFT // 2 + 3 * ((b - LEFT) // 4 + 1))))
                    if b >= 16:
                        pe.wait_ge(*done("aet_used", 7 * l + b // 4 - 3))
                    for n in range(b, min(b + 4, G)):
                        last = te.transpose(PS[b // 4 % 4][:, (n - b) * P:(n - b + 1) * P], LB[:, n * P:(n + 1) * P], ident[:, :])
                    last.then_inc(S["aet_ready"], 1)
                pe.wait_ge(*done("aet_used", 7 * (l + 1)))
                with pe.Fori(0, J // 2) as i:
                    for q in range(2):
                        for st in (1, 0):
                            u = 2 * st + q
                            pe.wait_ge(oh_ready[u], i + (l * (J // 2) + 1))
                            pe.wait_ge(pv_ready[u], i + (l * (J // 2) + 1))
                            for b in range(4):
                                tiles = (l * 8 * G + (q - 1) * HALF) + min(4 * b + 4, HALF)
                                if st == 0:
                                    pe.wait_ge(*done("act_col", i * (2 * G) + 2 * tiles))
                                else:
                                    pe.wait_ge(*done("sum1_added", i * G + tiles))
                                for m in range(4 * b, min(4 * b + 4, HALF)):
                                    last = te.matmul(PS[4 * st + b][:, m % 4 * P:(m % 4 + 1) * P],
                                                     V4[u][:, m * P:(m + 1) * P], OH4[u][:, m * P:(m + 1) * P], start=True, stop=True)
                                last.then_inc(S[f"sum{st}_ready"], 1)
                pe.wait_ge(*done("act_col", 16 * G * (l + 1)))
                pe.wait_ge(*done("sum1_added", 8 * G * (l + 1)))
                pe.wait_ge(*done("bias_made", 2))

                def attend(n, k):
                    pe.wait_ge(*done("sum_ready", n + (NB * l + 1)))
                    pe.wait_ge(*done("res_ready", n + (NB * l - 1)))
                    if l == 0:
                        te.matmul(PS[k][:, 0:P], ones3[:, :], bo, start=True, stop=False)
                        te.matmul(PS[k][:, 0:P], xn[k], Wo[:, :], start=False, stop=True).then_inc(S["att_ready"], 1)
                    else:
                        te.transpose(PS[k][:, 0:P], xn[k], ident[:, :]).then_inc(S["att_ready"], 1)

                blocks(pe, attend)
                pe.wait_ge(*done("res_ready", NB * (l + 1)))

                def turn2(n, k):
                    if l == 0:
                        pe.wait_ge(*done("xn_ready", n + (NB + 1)))
                    else:
                        pe.wait_ge(*done("ln_affine", n * 3 + 2))
                    pe.wait_ge(*done("ht_ready", n + ((2 * l + 1) * NB - 1)))
                    te.transpose(PS[k][:, 0:P], (hN if l else xn)[k], ident[:, :]).then_inc(S["tp_ready"], 1)

                def widen(n, k):
                    pe.wait_ge(*done("ht_ready", n + ((2 * l + 1) * NB + 1)))
                    pe.wait_ge(*done("gelu_ready", n * 4 + (4 * NB * l - 4)))
                    for c in range(4):
                        last = te.matmul(PS[2 + k][:, c * P:(c + 1) * P], W1[l][:, c * P:(c + 1) * P], hT[k], start=True, stop=True)
                    last.then_inc(S["hidden_ready"], 1)

                def narrow(n, k):
                    pe.wait_ge(*done("gelu_ready", n * 4 + (4 * NB * l + 4)))
                    pe.wait_ge(*done("ffn_added", n + (NB * l - 1)))
                    o = PS[4 + k][:, 0:P]
                    te.matmul(o, ones3[:, :], bf2[l], start=True, stop=False)
                    for c in range(4):
                        last = te.matmul(o, gT[k][:, c, :], W2[l][:, c, :], start=False, stop=(c == 3))
                    last.then_inc(S["ffn_ready"], 1)

                pipelined(pe, (turn2, 2), (widen, 1), (narrow, 0))
                pe.wait_ge(*done("ffn_added", NB * (l + 1)))

        @block.vector
        def _(dve):
            v = nc.vector
            xc = [0]

            def scan(o, gate, data, init, op0, op1):
                return v.tensor_tensor_scan(o, gate, data, init, op0, op1)

            def exchange(forward, gate, op0, op1):
                xc[0] += 1
                dve.wait_ge(*done("xc_row", xc[0] + 1))
                if forward:
                    scan(srow[0:1, 0, 1:P + 1], grow[0:1, gate, :], PS[7][0:1, 0:P], 0.0, op0, op1).then_inc(S["xc_scanned"], 1)
                else:
                    scan(srow[0:1, 1, 0:P][:, ::-1], grow[0:1, gate, ::-1], PS[7][0:1, 0:P][:, ::-1], 0.0, op0, op1).then_inc(S["xc_scanned"], 1)
                dve.wait_ge(*done("xc_back", xc[0]))
                return v.tensor_copy(cols[:, 2:3], PS[7][:, P:P + 1])

            def block_stats(src, n):
                dve.wait_ge(S["x_loaded"], 16)
                v.bn_stats(BN[:, ds(n, 1), :].rearrange("p a c -> p (a c)"), src[:, ds(n * P, P)]).then_inc(S["stat_step"], 1)

            def inv_std(n):
                dve.wait_ge(*done("stat_step", NB * n))
                even, odd = BN[:, :, 1], BN[:, :, 4]
                v.tensor_tensor(MEAN[:, :], even, odd, ALU.add).then_inc(S["moment_step"], 1)
                v.tensor_tensor(SD[:, :], even, odd, ALU.subtract).then_inc(S["moment_step"], 1)
                v.tensor_tensor(RS[:, :], BN[:, :, 2], BN[:, :, 5], ALU.add).then_inc(S["moment_step"], 1)
                dve.wait_ge(*done("moment_step", 7 * n - 4))
                v.tensor_scalar(MEAN[:, :], MEAN[:, :], 0.5, None, ALU.mult).then_inc(S["moment_step"], 1)
                v.scalar_tensor_tensor(SD[:, :], SD[:, :], 0.25, SD[:, :], ALU.mult, ALU.mult).then_inc(S["moment_step"], 1)
                v.tensor_scalar(RS[:, :], RS[:, :], 1.0 / D, EPS, ALU.mult, ALU.add).then_inc(S["moment_step"], 1)
                dve.wait_ge(*done("moment_step", 7 * n - 1))
                v.tensor_tensor(RS[:, :], RS[:, :], SD[:, :], ALU.add).then_inc(S["moment_step"], 1)
                dve.wait_ge(*done("moment_step", 7 * n))
                dve.sem_inc(S["var_ready"], 1)
                dve.wait_ge(*done("sd_ready", n))
                v.reciprocal(RS[:, :], SD[:, :]).then_inc(S["rs_ready"], 1)
                dve.wait_ge(*done("rs_ready", n))

            def normalise(o, src, n):
                return v.tensor_scalar(o, src[:, ds(n * P, P)], MEAN[:, ds(n, 1)], RS[:, ds(n, 1)], ALU.subtract, ALU.mult)

            dve.wait_ge(S["dstg_loaded"], 16)
            g3 = dstG.rearrange("g (j e) -> g j e", j=J)
            v.tensor_scalar(blkG, g3[:, :, 0], 7, 7, ALU.logical_shift_right, ALU.logical_shift_left).then_inc(S["rel_made"], 1)
            dve.wait_ge(*done("rel_made", 1))
            v.tensor_tensor(relG.rearrange("g (j e) -> g j e", j=J), g3, blkG.unsqueeze(2).broadcast_to([G, J, P]), ALU.subtract)\
                .then_inc(S["rel_made"], 1)
            dve.wait_ge(S["dste_loaded"], 32)
            v.tensor_tensor(rel_edge[:, :], dst_edge, dst_first[:, :], ALU.subtract).then_inc(S["rel_made"], 1)
            dve.wait_ge(S["x_loaded"], 16)
            blocks(dve, lambda n, k: block_stats(X, n), unroll=6)
            bias = Steps(dve, "bias_step")

            def split_biases(first, end):
                c, w = slice(first * D, end * D), (end - first) * D
                raw, parts = bias_raw[:, c], BIAS[:, c]
                hi, mid, lo, rest = bias_hi[:, 0:w], bias_mid[:, 0:w], bias_lo[:, 0:w], bias_rest[:, 0:w]
                bias.run(v.tensor_copy(hi, raw))
                bias.run(v.tensor_tensor(rest, raw, hi, ALU.subtract))
                bias.run(v.tensor_copy(mid, rest))
                bias.run(v.tensor_tensor(lo, rest, mid, ALU.subtract))
                bias.run(v.tensor_scalar(parts, hi, ident[0:3, 0:1], None, ALU.mult))
                bias.run(v.scalar_tensor_tensor(parts, mid, ident[0:3, 1:2], parts, ALU.mult, ALU.add))
                bias.run(v.scalar_tensor_tensor(parts, lo, ident[0:3, 2:3], parts, ALU.mult, ALU.add))
                dve.sem_inc(S["bias_made"], 1)

            dve.wait_ge(S["first_weights"], 16 * FIRST_WEIGHTS)
            dve.wait_ge(*done("consts_made", 10))
            split_biases(0, 3)
            inv_std(1)
            prep = Steps(dve, "prep_step")

            def gates(i):
                c0, width = i * (CH // 8), CH // 8
                at, here = ds(c0, width), dstB[:, ds(c0 + 1, width)]
                v.tensor_tensor(SAME_P[:, at], dstB[:, at], here, ALU.is_equal).then_inc(S["gates_made"], 1)
                v.tensor_tensor(SAME_N[:, at], here, dstB[:, ds(c0 + 2, width)], ALU.is_equal).then_inc(S["gates_made"], 1)
                v.tensor_tensor(is_loop[:, at], srcB[:, at], here, ALU.is_equal).then_inc(S["gates_made"], 1)
                dve.wait_ge(*done("gates_made", i * 5 + 2))
                v.tensor_scalar(ADD_P[:, at], SAME_P[:, at], 1.0, BIG, ALU.subtract, ALU.mult).then_inc(S["gates_made"], 1)
                v.tensor_scalar(ADD_N[:, at], SAME_N[:, at], 1.0, BIG, ALU.subtract, ALU.mult).then_inc(S["gates_made"], 1)

            def count_loops():
                dve.wait_ge(*done("gates_made", 40))
                prep.run(v.tensor_reduce(cols[:, 0:1], SAME_P[:, :], AX.X, ALU.min))
                prep.run(v.tensor_reduce(cols[:, 1:2], SAME_N[:, :], AX.X, ALU.min))
                prep.run(scan(loops, SAME_P[:, :], is_loop[:, :], 0.0, ALU.mult, ALU.add))

            def first_loops():
                dve.wait_ge(*done("xc_row", 1))
                prep.run(v.tensor_copy(grow[:, 0:2, :].rearrange("a b n -> a (b n)"), PS[7][0:1, 0:2 * P]))
                dve.sem_inc(S["xc_col"], 1)
                prep.run(v.tensor_scalar(grow[:, 2:4, :], grow[:, 0:2, :], 1.0, BIG, ALU.subtract, ALU.mult))
                prep.run(exchange(True, 0, ALU.mult, ALU.add))
                prep.run(scan(loops, SAME_P[:, :], is_loop[:, :], cols[:, 2:3], ALU.mult, ALU.add))
                prep.run(v.scalar_tensor_tensor(LOOP1[:, :], loops, 1.0, is_loop[:, :], ALU.is_equal, ALU.mult))

            for l in range(2):
                soft = Steps(dve, "soft_step")
                soft.base = SOFT * l
                def normal(n, k):
                    dve.wait_ge(*done("tp_ready", n + (2 * NB * l - 1)))
                    if l:
                        dve.wait_ge(*done("x_kept", n - 1))
                    normalise(xn[k], X, n).then_inc(S["xn_ready"], 1)

                def queries(n, k):
                    at = ds(n * P, P)
                    dve.wait_ge(*done("proj_ready", n + (NB * l + 1)))
                    if l:
                        dve.wait_ge(*done("x_kept", n + 1))
                        v.tensor_tensor(Y[:, at], PS[2 + k][:, 3 * D:4 * D], X[:, at], ALU.add).then_inc(S["batch_step"], 1)
                    v.tensor_scalar(QT[:, at], PS[2 + k][:, 0:D], 0.25, None, ALU.mult).then_inc(S["q_made"], 1)

                pipelined(dve, (normal, 3), (queries, 0))
                if l:
                    dve.wait_ge(*done("batch_step", NB))
                    dve.wait_ge(*done("x_kept", NB))
                dve.wait_ge(S["rel_stored"], 32)
                def one_hots1(n, s):
                    dve.wait_ge(rel_loaded[s], n * 8 + (16 * PAIRS * l + 16 - 8 * s))
                    dve.wait_ge(*done("qe_ready", n * 4 + (8 * PAIRS * l - 2)))
                    for nf in range(2):
                        v.tensor_scalar(OHT[:, 0, nf, :], REL[:, s, 0:8 * P], iota_part[:, nf:nf + 1], None,
                                        ALU.is_equal).then_inc(S["oht_ready"], 1)

                def logits(i, s, last=False):
                    def add_products(q4):
                        dve.wait_ge(*done("prod_done", i * 8 + (8 * PAIRS * l + 4 * s + q4 + 1)))
                        if q4 == 0:
                            dve.wait_ge(*done("lt_ready", i * 2 + (NB * l + s - 1)))
                        v.tensor_reduce(Ls[s].rearrange("p (h j) -> p j h", h=H)[:, 4 * q4:4 * q4 + 4, :],
                                        prod[q4].rearrange("p (j h c) -> p j h c", j=4, h=H), AX.X, ALU.add).then_inc(S["l_ready"], 1)

                    if not last:
                        one_hots1(i * 2 + (s + 1), 1 - s)
                    for q4 in range(4):
                        kk = KV[:, s, 4 * q4:4 * q4 + 4, 0:D]
                        if q4 % 2 == 0:
                            dve.wait_ge(gathered[s][q4 // 2], i * HALF_BATCH + HALF_BATCH * (PAIRS * l + 1))
                        if l:
                            dve.wait_ge(*done("e_ready", i * 8 + (4 * s + q4 + 1)))
                            ep = PS[4 + q4 % 2][:, :].rearrange("p (j d) -> p j d", j=4)
                            vv = KV[:, s, 4 * q4:4 * q4 + 4, D:2 * D]
                            v.tensor_tensor(kk, kk, ep, ALU.add).then_inc(S["batch_step"], 1)
                            v.tensor_tensor(vv, vv, ep, ALU.add).then_inc(S["e_used"], 1)
                            dve.wait_ge(*done("batch_step", i * 8 + (NB + 4 * s + q4 + 1)))
                        dve.wait_ge(*done("qe_ready", i * 8 + (8 * PAIRS * l + 4 * s + q4 + 1)))
                        dve.wait_ge(*done("l_ready", i * 8 + (8 * PAIRS * l + 4 * s + q4 - 3)))
                        v.tensor_tensor(prod[q4].rearrange("p (j d) -> p j d", j=4), kk, PS[q4][:, :].rearrange("p (j d) -> p j d", j=4),
                                        ALU.mult).then_inc(S["prod_done"], 1)
                        if q4:
                            add_products(q4 - 1)
                    add_products(3)

                def batches(first, end, also=None):
                    with dve.Fori(first, end) as i:
                        for s in range(2):
                            logits(i, s)
                        if also:
                            also(i)

                if l == 0:
                    split_biases(3, 10)
                one_hots1(0, 0)
                if l == 0:
                    dve.wait_ge(S["chunks_loaded"], 16 * 2 * H)
                    batches(0, 8, gates)
                    count_loops()
                    batches(8, 10)
                    first_loops()
                batches(10 if l == 0 else 0, PAIRS - 1)
                logits(PAIRS - 1, 0)
                logits(PAIRS - 1, 1, last=True)
                dve.wait_ge(*done("lb_ready", NB * (l + 1)))
                dve.sem_inc(S["logits_done"], 1)
                F1 = FB[:, :]
                scan(F1, ADD_P[:, :], LB[:, :], -BIG, ALU.add, ALU.max).then_inc(S["xc_col"], 1)
                rev = lambda x: x[:, ::-1]
                soft.run(exchange(True, 2, ALU.add, ALU.max))
                soft.run(scan(F1, ADD_P[:, :], LB[:, :], cols[:, 2:3], ALU.add, ALU.max))
                scan(rev(MB[:, :]), rev(ADD_N[:, :]), rev(F1), -BIG, ALU.add, ALU.max).then_inc(S["xc_col"], 1)
                soft.run(exchange(False, 3, ALU.add, ALU.max))
                soft.run(scan(rev(MB[:, :]), rev(ADD_N[:, :]), rev(F1), cols[:, 2:3], ALU.add, ALU.max))
                parts = [slice(p * QUARTER, (p + 1) * QUARTER) for p in range(4)]
                for c in parts:
                    v.tensor_tensor(LB[:, c], LB[:, c], MB[:, c], ALU.subtract).then_inc(S["shifted"], 1)
                for p, c in enumerate(parts):
                    dve.wait_ge(*done("exp_ready", 4 * l + p + 1))
                    if l == 0:
                        soft.run(v.scalar_tensor_tensor(LB[:, c], LOOP1[:, c], 1.0, LB[:, c], ALU.add, ALU.mult))
                    else:
                        dve.sem_inc(S["soft_step"], 1)
                        soft.n += 1
                    part = scan(F1[:, c], SAME_P[:, c], LB[:, c], FB[:, p * QUARTER - 1:p * QUARTER] if p else 0.0, ALU.mult, ALU.add)
                    if p < 3:
                        soft.run(part)
                    else:
                        part.then_inc(S["xc_col"], 1)
                soft.run(exchange(True, 0, ALU.mult, ALU.add))
                soft.run(scan(F1, SAME_P[:, :], LB[:, :], cols[:, 2:3], ALU.mult, ALU.add))
                scan(rev(MB[:, :]), rev(SAME_N[:, :]), rev(F1), 0.0, ALU.mult, ALU.max).then_inc(S["xc_col"], 1)
                soft.run(exchange(False, 1, ALU.mult, ALU.max))
                left, right = slice(0, LEFT * P), slice(LEFT * P, CH)
                soft.run(scan(rev(MB[:, right]), rev(SAME_N[:, right]), rev(FB[:, right]), cols[:, 2:3], ALU.mult, ALU.max))
                soft.run(scan(rev(MB[:, left]), rev(SAME_N[:, left]), rev(FB[:, left]), MB[:, LEFT * P:LEFT * P + 1], ALU.mult, ALU.max))
                assert soft.n == SUMS
                for b in range(0, LEFT, 4):
                    c = slice(b * P, (b + 4) * P)
                    soft.run(v.reciprocal(MB[:, c], MB[:, c]))
                    soft.run(v.tensor_tensor(LB[:, c], LB[:, c], MB[:, c], ALU.mult))
                dve.wait_ge(*done("inverse_step", 2 * l + 2))
                for b in range(LEFT, G, 4):
                    c = slice(b * P, min(b + 4, G) * P)
                    soft.run(v.tensor_tensor(MB[:, c], MB[:, c], FB[:, c], ALU.mult))
                    soft.run(v.scalar_tensor_tensor(MB[:, c], MB[:, c], 2.0, FB[:, c], ALU.subtract, ALU.mult))
                    soft.run(v.scalar_tensor_tensor(LB[:, c], MB[:, c], -1.0, LB[:, c], ALU.mult, ALU.mult))
                assert soft.n == SOFT
                dve.wait_ge(*done("agg_zeroed", 3 * (l + 1)))

                def one_hots(i, q):
                    for st in (1, 0):
                        u = 2 * st + q
                        if st == 0:
                            dve.wait_ge(*done("aet_ready", 7 * (l + 1)))
                        dve.wait_ge(*done(f"sum{st}_ready", i * 8 + (64 * l + 4 * q - 4)))
                        v.tensor_tensor(OH4[u].rearrange("p (m n) -> p m n", m=HALF),
                                        iota_row[:, :].unsqueeze(1).broadcast_to([P, HALF, P]),
                                        rel_edge[:, ds(i * G + (st * 8 * G + q * HALF), HALF)].unsqueeze(2).broadcast_to([P, HALF, P]),
                                        ALU.is_equal).then_inc(oh_ready[u], 1)

                def add_up(i, q):
                    for m in range(HALF):
                        n = q * HALF + m
                        if m == 0:
                            firsts = values(first_row, i * 32 + (16 * J + q * 16), HALF, ENG.DVE, N)
                        if m % 4 == 0:
                            dve.wait_ge(*done("sum1_ready", i * 8 + (l * 64 + q * 4 + m // 4 + 1)))
                        dve.wait_ge(*done("sum1_added", i * G + (l * 8 * G + n - 1)))
                        at = AGG[1 + n % 2][:, ds(firsts[m], P)]
                        v.tensor_tensor(at, at, PS[4 + m // 4][:, m % 4 * P:(m % 4 + 1) * P], ALU.add).then_inc(S["sum1_added"], 1)

                last = J // 2 - 1
                one_hots(0, 0)
                with dve.Fori(0, last) as i:
                    one_hots(i, 1)
                    add_up(i, 0)
                    one_hots(i + 1, 0)
                    add_up(i, 1)
                one_hots(last, 1)
                add_up(last, 0)
                add_up(last, 1)
                dve.wait_ge(*done("act_col", 16 * G * (l + 1)))
                dve.wait_ge(*done("sum1_added", 8 * G * (l + 1)))
                def add_streams(n, k):
                    at = ds(n * P, P)
                    dve.wait_ge(*done("att_ready", n + (NB * l - 1)))
                    dve.wait_ge(*done("half_sum", n + (NB * l + 1)))
                    v.tensor_tensor(xn[k], QT[:, at], AG1[:, at], ALU.add).then_inc(S["sum_ready"], 1)

                def residual(n, k):
                    at = ds(n * P, P)
                    dve.wait_ge(*done("att_ready", n + (NB * l + 1)))
                    v.tensor_tensor(Y[:, at], PS[k][:, 0:P], (Y if l else X)[:, at], ALU.add).then_inc(S["res_ready"], 1)

                def residual_stats(n, k):
                    dve.wait_ge(*done("res_ready", n + (NB * l + 1)))
                    block_stats(Y, n)

                pipelined(dve, (add_streams, 3), (residual, 1), (residual_stats, 0))
                inv_std(2 if l == 0 else 4)

                def normal2(n, k):
                    if l == 0:
                        dve.wait_ge(*done("tp_ready", n + (NB - 1)))
                        normalise(xn[k], Y, n).then_inc(S["xn_ready"], 1)
                    else:
                        normalise(Y[:, ds(n * P, P)], Y, n).then_inc(S["xn_ready"], 1)

                def turned2(n, k):
                    dve.wait_ge(*done("tp_ready", n + ((2 * l + 1) * NB + 1)))
                    dve.wait_ge(*done("hidden_ready", n + (NB * l - 1)))
                    if l == 0:
                        v.tensor_scalar(hT[k], PS[k][:, 0:P], gb[:, 2:3], gb[:, 3:4], ALU.mult, ALU.add).then_inc(S["ht_ready"], 1)
                    else:
                        v.tensor_copy(hT[k], PS[k][:, 0:P]).then_inc(S["ht_ready"], 1)

                def add_ffn(n, k):
                    at = ds(n * P, P)
                    dve.wait_ge(*done("ffn_ready", n + (NB * l + 1)))
                    if l == 0:
                        dve.wait_ge(*done("x_summed", n + 1))
                        v.tensor_tensor(X[:, at], PS[4 + k][:, 0:P], X[:, at], ALU.add).then_inc(S["ffn_added"], 1)
                    else:
                        dve.wait_ge(*done("ln_affine", n * 3 + 3))
                        v.tensor_tensor(Y[:, at], PS[4 + k][:, 0:P], Y[:, at], ALU.add).then_inc(S["ffn_added"], 1)

                def ffn_stats(n, k):
                    dve.wait_ge(*done("ffn_added", n + (NB * l + 1)))
                    block_stats(Y if l else X, n)

                pipelined(dve, (normal2, 7 if l else 4), (turned2, 3), (add_ffn, 1), (ffn_stats, 0))
                inv_std(3 if l == 0 else 5)

            dve.wait_ge(*done("x_shifted", 1))

            def normal3(n, k):
                dve.wait_ge(*done("ln_last", n - 1))
                normalise(xn[k], Y, n).then_inc(S["xn_ready"], 1)

            def add_input(n, k):
                at = ds(n * P, P)
                dve.wait_ge(*done("ln_last", n + 1))
                v.tensor_tensor(X[:, at], X[:, at], hN[k], ALU.add).then_inc(S["x_out"], 1)

            def out_stats(n, k):
                dve.wait_ge(*done("x_out", n + 1))
                block_stats(X, n)

            pipelined(dve, (normal3, 3), (add_input, 1), (out_stats, 0))
            inv_std(6)
            v.scalar_tensor_tensor(SD[:, :], MEAN[:, :], -1.0, RS[:, :], ALU.mult, ALU.mult).then_inc(S["shift_made"], 1)
            blocks(dve, lambda n, k: normalise(Y[:, ds(n * P, P)], X, n).then_inc(S["out_made"], 1), end=DVE_OUT)


DVE_OUT = 14
QUARTER = CH // 4
LEFT = 4
SUMS = 16
SOFT = SUMS + 20
FIRST_WEIGHTS = 17
WEIGHTS = 22

_SHAPED = ["L0_gnn_Wq", "L0_gnn_bq", "L0_gnn_Wk", "L0_gnn_bk", "L0_gnn_Wv", "L0_gnn_bv", "L0_gnn_Wo", "L0_gnn_bo",
           "L0_gnn_g1", "L0_gnn_b1", "L0_gnn_g2", "L0_gnn_b2", "L0_gnn_W1", "L0_gnn_bf1", "L0_gnn_W2", "L0_gnn_bf2",
           "L1_gnn_Wq", "L1_gnn_bq", "L1_gnn_Wk", "L1_gnn_bk", "L1_gnn_Wv", "L1_gnn_bv", "L1_gnn_We", "L1_gnn_Wskip",
           "L1_gnn_bskip", "L1_gnn_g1", "L1_gnn_b1", "L1_gnn_g2", "L1_gnn_b2", "L1_gnn_Wf1", "L1_gnn_bf1",
           "L1_gnn_Wf2", "L1_gnn_bf2"]


def kernel(**inputs):
    import numpy as np
    import concourse.bacc as bacc
    from concourse.bass_utils import run_bass_kernel_spmd as run

    nc = bacc.Bacc("TRN2", target_bir_lowering=False, num_devices=1)
    src = np.zeros(EP, np.int32)
    src[:E] = inputs["src"]
    dst = np.full(EP + 2, N, np.int32)
    dst[0] = -1
    dst[EP + 1] = N + 1
    dst[1:E + 1] = inputs["dst"]
    x = np.zeros((NP, D), np.float32)
    x[:N] = inputs["x"]
    edges = np.zeros((EP, ED), np.float32)
    edges[:E] = inputs["edge_attr_64"]
    arrays = {
        "x": x,
        "src": src,
        "dst": dst,
        "src_batch": np.ascontiguousarray(src.reshape(J, G, P).transpose(1, 2, 0)),
        "dst_edge": np.ascontiguousarray(dst[1:EP + 1].reshape(T, P).T),
        "dst_first": np.ascontiguousarray(dst[1:EP + 1].reshape(T, P)[:, 0]),
        "edge_batch": np.ascontiguousarray(edges.reshape(J, G, P, ED).transpose(1, 3, 0, 2)).reshape(G, ED, J * P),
    }
    for name in _SHAPED:
        arrays[name] = np.ascontiguousarray(inputs[name])
    units = np.full((2 * J, 16), N, np.int32)
    units[:, :HALF] = arrays["dst_first"].reshape(2 * J, HALF)
    arrays["dst_units"] = units.reshape(-1)
    a = {}
    for name, v in arrays.items():
        dt = U32 if name == "src_batch" else mybir.dt.from_np(v.dtype)
        a[name] = nc.dram_tensor(f"in_{name}", v.shape, dt, kind="ExternalInput").ap()
    out = nc.dram_tensor("out_0", (N, D), F32, kind="ExternalOutput").ap()
    build(nc, a, out)
    r = run(nc, [{f"in_{k}": v for k, v in arrays.items()}], core_ids=[0])
    return r.results[0]["out_0"]
```
